# Optimizing a Trainium2 kernel written in Bass

```python
import numpy as np
import jax
import jax.numpy as jnp

def _softmax(x, axis=-1):
    return jax.nn.softmax(x, axis=axis)

def _gelu(x):
    return jax.nn.gelu(x, approximate=True)

def _silu(x):
    return jax.nn.silu(x)

def _sigmoid(x):
    return jax.nn.sigmoid(x)

def _layernorm(x, axis=-1, eps=1e-05):
    m = jnp.mean(x, axis=axis, keepdims=True)
    v = jnp.var(x, axis=axis, keepdims=True)
    return (x - m) / jnp.sqrt(v + eps)

def _scatter_add(tgt, idx, src, axis=0):
    return tgt.at[idx].add(src)

def _segment_sum(src, seg, n):
    return jax.ops.segment_sum(src, seg, n)
kernel_name = 'mk_gnn_resnorm_d4_gnn_r8_716dd4'

def setup_inputs(seed: int=0):
    np.random.seed(seed)
    _w = jnp.asarray

    def _rec_inputs():
        import jax
        import jax.numpy as jnp
        _gk = jax.random.key(seed)
        x = -0.0005121 + 1.001 * jax.random.normal(jax.random.fold_in(_gk, 1), (6250, 64), jnp.float32)
        src = jax.random.randint(jax.random.fold_in(_gk, 2), (200000,), 0, 6250, jnp.int32)
        dst = jax.random.randint(jax.random.fold_in(_gk, 3), (200000,), 0, 6250, jnp.int32)
        _o = jnp.argsort(dst, stable=True)
        src = src[_o]
        dst = dst[_o]
        edge_attr_128 = jax.random.uniform(jax.random.fold_in(_gk, 12), (200000, 128), jnp.float32, 0.0, 1)
        edge_attr_16 = 0.000254156 + 0.999948 * jax.random.normal(jax.random.fold_in(_gk, 13), (200000, 16), jnp.float32)
        edge_attr_64 = -9.77346e-05 + 0.999888 * jax.random.normal(jax.random.fold_in(_gk, 14), (200000, 64), jnp.float32)
        return (x, src, dst, edge_attr_128, edge_attr_16, edge_attr_64)
    x, src, dst, edge_attr_128, edge_attr_16, edge_attr_64 = _rec_inputs()

    def _L0_gnn_setup():
        import jax, jax.numpy as jnp
        import numpy as np
        N = 6250
        E = 100000
        D = 64
        key = jax.random.key(seed)
        k1, k2, k3, k4, k5, k6 = jax.random.split(key, 6)
        node_feats = jax.random.normal(k1, (N, D), dtype=jnp.float32)
        edge_feats = jax.random.normal(k2, (E, D), dtype=jnp.float32)
        src = jax.random.randint(k3, (E,), 0, N, dtype=jnp.int32)
        dst = jnp.sort(jax.random.randint(k4, (E,), 0, N, dtype=jnp.int32))
        lim = 1.0 / np.sqrt(D)
        W = jax.random.uniform(k5, (D, D), minval=-lim, maxval=lim, dtype=jnp.float32)
        b = jax.random.uniform(k6, (D,), minval=-lim, maxval=lim, dtype=jnp.float32)
        return {'node_feats': node_feats, 'edge_feats': edge_feats, 'src': src, 'dst': dst, 'W': W, 'b': b}
    _L0_gnn_all = _L0_gnn_setup()
    _L0_gnn_in = {k: v for k, v in _L0_gnn_all.items() if k in ('W', 'b')}
    del _L0_gnn_all

    def _L1_gnn_setup():
        import jax, jax.numpy as jnp
        import numpy as np
        N_NODES = 6250
        N_EDGES = 100000
        IN_CH = 64
        HID_CH = 64

        def _gcn_conv(x, src, dst, W, b, num_nodes):
            h = x @ W
            loops = jnp.arange(num_nodes, dtype=src.dtype)
            s = jnp.concatenate([src, loops])
            d = jnp.concatenate([dst, loops])
            deg = jax.ops.segment_sum(jnp.ones_like(d, dtype=h.dtype), d, num_segments=num_nodes)
            dinv = jnp.where(deg > 0, jax.lax.rsqrt(deg), 0.0)
            norm = dinv[s] * dinv[d]
            msg = h[s] * norm[:, None]
            out = jax.ops.segment_sum(msg, d, num_segments=num_nodes)
            return out + b
        key = jax.random.key(seed)
        k1, k2, k3, k4, k5, k6 = jax.random.split(key, 6)
        x = jax.random.normal(k1, (N_NODES, IN_CH), dtype=jnp.float32)
        edge_index = jax.random.randint(k2, (2, N_EDGES), 0, N_NODES, dtype=jnp.int32)
        W1 = jax.random.normal(k3, (IN_CH, HID_CH), dtype=jnp.float32) * (1.0 / np.sqrt(IN_CH))
        b1 = jax.random.normal(k4, (HID_CH,), dtype=jnp.float32) * 0.01
        W2 = jax.random.normal(k5, (HID_CH, HID_CH), dtype=jnp.float32) * (1.0 / np.sqrt(HID_CH))
        b2 = jax.random.normal(k6, (HID_CH,), dtype=jnp.float32) * 0.01
        return {'x': x, 'edge_index': edge_index, 'W1': W1, 'b1': b1, 'W2': W2, 'b2': b2}
    _L1_gnn_all = _L1_gnn_setup()
    _L1_gnn_in = {k: v for k, v in _L1_gnn_all.items() if k in ('W1', 'b1', 'W2', 'b2')}
    del _L1_gnn_all

    def _L2_gnn_setup():
        import jax, jax.numpy as jnp
        import numpy as np
        EPS = 1e-05

        def _batchnorm(x, w, b):
            mean = jnp.mean(x, axis=0)
            var = jnp.mean((x - mean) ** 2, axis=0)
            return (x - mean) * jax.lax.rsqrt(var + EPS) * w + b
        key = jax.random.key(seed)
        ks = jax.random.split(key, 8)
        N, E, F, G = (12500, 200000, 64, 128)
        atom_fea = jax.random.normal(ks[0], (N, F), dtype=jnp.float32)
        edge_fea = jax.random.uniform(ks[1], (E, G), dtype=jnp.float32)
        fc_w = jax.random.normal(ks[2], (2 * F, 2 * F + G), dtype=jnp.float32) / np.sqrt(2 * F + G)
        fc_b = jax.random.normal(ks[3], (2 * F,), dtype=jnp.float32) * 0.01
        bn1_w = jax.random.uniform(ks[4], (2 * F,), dtype=jnp.float32) + 0.5
        bn1_b = jax.random.normal(ks[5], (2 * F,), dtype=jnp.float32) * 0.01
        bn2_w = jax.random.uniform(ks[6], (F,), dtype=jnp.float32) + 0.5
        bn2_b = jax.random.normal(ks[7], (F,), dtype=jnp.float32) * 0.01
        src = jax.random.randint(jax.random.fold_in(key, 100), (E,), 0, N, dtype=jnp.int64)
        dst = jax.random.randint(jax.random.fold_in(key, 101), (E,), 0, N, dtype=jnp.int64)
        return {'atom_fea': atom_fea, 'edge_fea': edge_fea, 'fc_w': fc_w, 'fc_b': fc_b, 'bn1_w': bn1_w, 'bn1_b': bn1_b, 'bn2_w': bn2_w, 'bn2_b': bn2_b, 'src': src, 'dst': dst}
    _L2_gnn_all = _L2_gnn_setup()
    _L2_gnn_in = {k: v for k, v in _L2_gnn_all.items() if k in ('fc_w', 'fc_b', 'bn1_w', 'bn1_b', 'bn2_w', 'bn2_b')}
    del _L2_gnn_all

    def _L3_gnn_setup():
        import jax, jax.numpy as jnp
        import numpy as np
        N, E, F, ED, L = (6250, 100000, 64, 16, 2)
        EPS_BN = 1e-05

        def _layer(x, src, dst, edge_attr, We, be, Wpre, bpre, Wpost, bpost, Wlin, blin, gamma, beta):
            e = edge_attr @ We + be
            h = jnp.concatenate([x[src], e], axis=-1) @ Wpre + bpre
            cnt = jax.ops.segment_sum(jnp.ones(h.shape[0], h.dtype), dst, num_segments=N)
            safe_cnt = jnp.maximum(cnt, 1.0)
            mean = jax.ops.segment_sum(h, dst, num_segments=N) / safe_cnt[:, None]
            empty = (cnt == 0)[:, None]
            mn = jnp.where(empty, 0.0, jax.ops.segment_min(h, dst, num_segments=N))
            mx = jnp.where(empty, 0.0, jax.ops.segment_max(h, dst, num_segments=N))
            agg = jnp.concatenate([mean, mn, mx], axis=-1)
            deg_i = cnt.astype(jnp.int32)
            bc = jnp.bincount(deg_i, length=N).astype(h.dtype)
            avg_log = jnp.mean(jnp.log(bc + 1.0))
            amp = (jnp.log(safe_cnt + 1.0) / avg_log)[:, None]
            out = jnp.concatenate([agg, agg * amp], axis=-1)
            out = jnp.concatenate([x, out], axis=-1) @ Wpost + bpost
            out = out @ Wlin + blin
            mu = out.mean(axis=0)
            var = jnp.mean((out - mu) ** 2, axis=0)
            out = gamma * (out - mu) / jnp.sqrt(var + EPS_BN) + beta
            return jax.nn.relu(out)
        key = jax.random.key(seed)
        ks = jax.random.split(key, 8)
        s = 0.05
        return {'x': jax.random.normal(ks[0], (N, F), jnp.float32), 'edge_index': jax.random.randint(ks[1], (2, E), 0, N), 'edge_attr': jax.random.normal(ks[2], (E, ED), jnp.float32), 'We': jax.random.normal(ks[3], (L, ED, F), jnp.float32) * s, 'be': jnp.zeros((L, F), jnp.float32), 'Wpre': jax.random.normal(ks[4], (L, 2 * F, F), jnp.float32) * s, 'bpre': jnp.zeros((L, F), jnp.float32), 'Wpost': jax.random.normal(ks[5], (L, 7 * F, F), jnp.float32) * s, 'bpost': jnp.zeros((L, F), jnp.float32), 'Wlin': jax.random.normal(ks[6], (L, F, F), jnp.float32) * s, 'blin': jnp.zeros((L, F), jnp.float32), 'gamma': jnp.ones((L, F), jnp.float32), 'beta': jnp.zeros((L, F), jnp.float32)}
    _L3_gnn_all = _L3_gnn_setup()
    _L3_gnn_in = {k: v for k, v in _L3_gnn_all.items() if k in ('We', 'be', 'Wpre', 'bpre', 'Wpost', 'bpost', 'Wlin', 'blin', 'gamma', 'beta')}
    del _L3_gnn_all
    return {'x': x, 'src': src, 'dst': dst, 'edge_attr_128': edge_attr_128, 'edge_attr_16': edge_attr_16, 'edge_attr_64': edge_attr_64, 'L0_gnn_W': _L0_gnn_in['W'], 'L0_gnn_b': _L0_gnn_in['b'], 'L1_gnn_W1': _L1_gnn_in['W1'], 'L1_gnn_b1': _L1_gnn_in['b1'], 'L1_gnn_W2': _L1_gnn_in['W2'], 'L1_gnn_b2': _L1_gnn_in['b2'], 'L2_gnn_fc_w': _L2_gnn_in['fc_w'], 'L2_gnn_fc_b': _L2_gnn_in['fc_b'], 'L2_gnn_bn1_w': _L2_gnn_in['bn1_w'], 'L2_gnn_bn1_b': _L2_gnn_in['bn1_b'], 'L2_gnn_bn2_w': _L2_gnn_in['bn2_w'], 'L2_gnn_bn2_b': _L2_gnn_in['bn2_b'], 'L3_gnn_We': _L3_gnn_in['We'], 'L3_gnn_be': _L3_gnn_in['be'], 'L3_gnn_Wpre': _L3_gnn_in['Wpre'], 'L3_gnn_bpre': _L3_gnn_in['bpre'], 'L3_gnn_Wpost': _L3_gnn_in['Wpost'], 'L3_gnn_bpost': _L3_gnn_in['bpost'], 'L3_gnn_Wlin': _L3_gnn_in['Wlin'], 'L3_gnn_blin': _L3_gnn_in['blin'], 'L3_gnn_gamma': _L3_gnn_in['gamma'], 'L3_gnn_beta': _L3_gnn_in['beta']}

def reference(x, src, dst, edge_attr_128, edge_attr_16, edge_attr_64, L0_gnn_W, L0_gnn_b, L1_gnn_W1, L1_gnn_b1, L1_gnn_W2, L1_gnn_b2, L2_gnn_fc_w, L2_gnn_fc_b, L2_gnn_bn1_w, L2_gnn_bn1_b, L2_gnn_bn2_w, L2_gnn_bn2_b, L3_gnn_We, L3_gnn_be, L3_gnn_Wpre, L3_gnn_bpre, L3_gnn_Wpost, L3_gnn_bpost, L3_gnn_Wlin, L3_gnn_blin, L3_gnn_gamma, L3_gnn_beta):
    import jax
    import jax.numpy as jnp

    def _L0_gnn_ref(node_feats, edge_feats, src, dst, W, b):
        import jax, jax.numpy as jnp
        import numpy as np
        N = 6250
        E = 100000
        D = 64
        m = node_feats[src] + edge_feats
        seg_max = jax.ops.segment_max(m, dst, num_segments=N)
        seg_max = jnp.where(jnp.isfinite(seg_max), seg_max, 0.0)
        ex = jnp.exp(m - seg_max[dst])
        denom = jax.ops.segment_sum(ex, dst, num_segments=N)
        a = ex / jnp.maximum(denom[dst], 1e-38)
        agg = jax.ops.segment_sum(m * a, dst, num_segments=N)
        out = jax.nn.relu(agg @ W.T + b) + node_feats
        return out

    def _L1_gnn_ref(x, edge_index, W1, b1, W2, b2):
        import jax, jax.numpy as jnp
        import numpy as np
        N_NODES = 6250
        N_EDGES = 100000
        IN_CH = 64
        HID_CH = 64

        def _gcn_conv(x, src, dst, W, b, num_nodes):
            h = x @ W
            loops = jnp.arange(num_nodes, dtype=src.dtype)
            s = jnp.concatenate([src, loops])
            d = jnp.concatenate([dst, loops])
            deg = jax.ops.segment_sum(jnp.ones_like(d, dtype=h.dtype), d, num_segments=num_nodes)
            dinv = jnp.where(deg > 0, jax.lax.rsqrt(deg), 0.0)
            norm = dinv[s] * dinv[d]
            msg = h[s] * norm[:, None]
            out = jax.ops.segment_sum(msg, d, num_segments=num_nodes)
            return out + b
        src, dst = (edge_index[0], edge_index[1])
        n = x.shape[0]
        h = jax.nn.relu(_gcn_conv(x, src, dst, W1, b1, n))
        return _gcn_conv(h, src, dst, W2, b2, n)

    def _L2_gnn_ref(atom_fea, edge_fea, fc_w, fc_b, bn1_w, bn1_b, bn2_w, bn2_b, src, dst):
        import jax, jax.numpy as jnp
        import numpy as np
        EPS = 1e-05

        def _batchnorm(x, w, b):
            mean = jnp.mean(x, axis=0)
            var = jnp.mean((x - mean) ** 2, axis=0)
            return (x - mean) * jax.lax.rsqrt(var + EPS) * w + b
        N, F = atom_fea.shape
        total = jnp.concatenate([atom_fea[dst], atom_fea[src], edge_fea], axis=1)
        total = _batchnorm(total @ fc_w.T + fc_b, bn1_w, bn1_b)
        gate, core = jnp.split(total, 2, axis=1)
        messages = jax.nn.sigmoid(gate) * jax.nn.softplus(core)
        aggr = jax.ops.segment_sum(messages, dst, num_segments=N)
        aggr = _batchnorm(aggr, bn2_w, bn2_b)
        return jax.nn.softplus(atom_fea + aggr)

    def _L3_gnn_ref(x, edge_index, edge_attr, We, be, Wpre, bpre, Wpost, bpost, Wlin, blin, gamma, beta):
        import jax, jax.numpy as jnp
        import numpy as np
        N, E, F, ED, L = (6250, 100000, 64, 16, 2)
        EPS_BN = 1e-05

        def _layer(x, src, dst, edge_attr, We, be, Wpre, bpre, Wpost, bpost, Wlin, blin, gamma, beta):
            e = edge_attr @ We + be
            h = jnp.concatenate([x[src], e], axis=-1) @ Wpre + bpre
            cnt = jax.ops.segment_sum(jnp.ones(h.shape[0], h.dtype), dst, num_segments=N)
            safe_cnt = jnp.maximum(cnt, 1.0)
            mean = jax.ops.segment_sum(h, dst, num_segments=N) / safe_cnt[:, None]
            empty = (cnt == 0)[:, None]
            mn = jnp.where(empty, 0.0, jax.ops.segment_min(h, dst, num_segments=N))
            mx = jnp.where(empty, 0.0, jax.ops.segment_max(h, dst, num_segments=N))
            agg = jnp.concatenate([mean, mn, mx], axis=-1)
            deg_i = cnt.astype(jnp.int32)
            bc = jnp.bincount(deg_i, length=N).astype(h.dtype)
            avg_log = jnp.mean(jnp.log(bc + 1.0))
            amp = (jnp.log(safe_cnt + 1.0) / avg_log)[:, None]
            out = jnp.concatenate([agg, agg * amp], axis=-1)
            out = jnp.concatenate([x, out], axis=-1) @ Wpost + bpost
            out = out @ Wlin + blin
            mu = out.mean(axis=0)
            var = jnp.mean((out - mu) ** 2, axis=0)
            out = gamma * (out - mu) / jnp.sqrt(var + EPS_BN) + beta
            return jax.nn.relu(out)
        src, dst = (edge_index[0], edge_index[1])
        for l in range(L):
            x = _layer(x, src, dst, edge_attr, We[l], be[l], Wpre[l], bpre[l], Wpost[l], bpost[l], Wlin[l], blin[l], gamma[l], beta[l])
        return x
    edge_index = jnp.stack([src, dst])
    x = _layernorm(x + _L0_gnn_ref(x, edge_attr_64, src, dst, L0_gnn_W, L0_gnn_b), axis=-1)
    x = _layernorm(x + _L1_gnn_ref(x, edge_index, L1_gnn_W1, L1_gnn_b1, L1_gnn_W2, L1_gnn_b2), axis=-1)
    x = _layernorm(x + _L2_gnn_ref(x, edge_attr_128, L2_gnn_fc_w, L2_gnn_fc_b, L2_gnn_bn1_w, L2_gnn_bn1_b, L2_gnn_bn2_w, L2_gnn_bn2_b, src, dst), axis=-1)
    x = _layernorm(x + _L3_gnn_ref(x, edge_index, edge_attr_16, L3_gnn_We, L3_gnn_be, L3_gnn_Wpre, L3_gnn_bpre, L3_gnn_Wpost, L3_gnn_bpost, L3_gnn_Wlin, L3_gnn_blin, L3_gnn_gamma, L3_gnn_beta), axis=-1)
    return x

_drawn_inputs = setup_inputs


def setup_inputs(seed=0):
    import zlib

    import numpy as np

    out = dict(_drawn_inputs(seed))
    spreads = {'L3_gnn_be': (0.0, 0.396),
     'L3_gnn_bpre': (0.0, 0.1),
     'L3_gnn_bpost': (0.0, 0.8),
     'L3_gnn_blin': (0.0, 0.8),
     'L3_gnn_gamma': (1.0, 0.2),
     'L3_gnn_beta': (0.0, 0.1)}
    factors = {'L1_gnn_b1': 8.0,
     'L1_gnn_b2': 4.899,
     'L2_gnn_fc_b': 8.0,
     'L2_gnn_bn1_b': 8.0,
     'L2_gnn_bn2_b': 8.0}
    for name, (base, spread) in spreads.items():
        noise = np.random.default_rng([zlib.crc32(name.encode()), seed]).standard_normal(out[name].shape)
        drawn = base * np.exp(spread * noise) if base else spread * noise
        out[name] = jnp.asarray(drawn.astype(out[name].dtype))
    for name, factor in factors.items():
        out[name] = (out[name] * factor).astype(out[name].dtype)
    return out
```

```python
import concourse.bass as bass
from concourse import mybir
from contextlib import ExitStack

N, E, F = 6250, 200000, 64
P = 128
NT = -(-N // P)
NP = NT * P
LAST = N - (NT - 1) * P
J = 4
BLK = P * J
U = 4
NB = -(-(-(-(E // 2) // BLK)) // U) * U
H = NB * BLK
IT = NB // U
BASE1 = E - H
OVER = H - BASE1
BIG = 3e38
SOFT, GCN1, GCN2, STAT, MSG, PNA1, PNA2 = range(7)
GATHER = (SOFT, GCN1, GCN2, STAT, PNA1, PNA2)
SCANS = (SOFT, GCN1, GCN2, MSG, PNA1, PNA2)
PNA = (PNA1, PNA2)
UNITS = {SOFT: 3, GCN1: 1, GCN2: 1, MSG: 1, PNA1: 3, PNA2: 3}
GS = 4
GROUPS = [(a, min(a + GS, NT)) for a in range(0, NT, GS)]
NG = len(GROUPS)


class Ring:

    def __init__(self, sem, name, adds):
        self.sems = [sem(f"{name}{u}") for u in range(U)]
        self.adds, self.base, total = adds, {}, 0
        for p in range(7):
            self.base[p] = total
            total += adds.get(p, 0) * IT

    def done(self, engine, p, i, u, back=0):
        own = u >= back
        value = i * self.adds[p] + (self.base[p] + self.adds[p] * own)
        if not (isinstance(value, int) and value <= 0):
            engine.wait_ge(self.sems[u - back if own else u - back + U], value)

    def all_done(self, engine, p):
        for u in range(U):
            engine.wait_ge(self.sems[u], self.base[p] + IT * self.adds[p])


def gnn_kernel(nc, x, src, dst, ea128, ea16, ea64, W0, b0, W1, b1, W2, b2, fcw, fcb, bn1w, bn1b,
               bn2w, bn2b, We, be, Wpre, bpre, Wpost, bpost, Wlin, blin, gamma, beta, out):
    f32, bf16, i32, u16 = mybir.dt.float32, mybir.dt.bfloat16, mybir.dt.int32, mybir.dt.uint16
    ALU, ACT, AX = mybir.AluOpType, mybir.ActivationFunctionType, mybir.AxisListType
    dram = lambda name, shape, dt=f32: nc.dram_tensor(name, shape, dt, kind="Internal").ap()
    keep_d = dram("keep_d", (2, H), bf16)
    table_d = [dram(f"table_d{p}", (NP, F)) for p in range(4)]
    tsrc_d, tdst_d = dram("tsrc_d", (NP, 2 * F)), dram("tdst_d", (NP, 2 * F))
    runs1_d, runs3_d = dram("runs1_d", (2 * H, F)), dram("runs3_d", (2 * H, 3 * F))
    seed_d = dram("seed_d", (2 * H, 2 * F))
    total_d = dram("total_d", (NB, P, 2, BLK))

    ctx = ExitStack()
    with ctx:
        sb = lambda name, shape, dt=f32: ctx.enter_context(nc.sbuf_tensor(name, shape, dt))
        pb = lambda name, shape, dt=f32: ctx.enter_context(nc.psum_tensor(name, shape, dt))
        sem = lambda name: ctx.enter_context(nc.semaphore(name))

        ident, onesN = sb("ident", [P, P]), sb("onesN", [P, P])
        tri, ones = sb("tri", [P, P]), sb("ones", [P, P])
        valid = sb("valid", [P, 1])
        src_all = sb("src_all", [P, 2, NB, J], u16)
        dlo, dhi = sb("dlo", [P, 2, NB, J], bf16), sb("dhi", [P, 2, NB, J], bf16)
        iota = sb("iota", [P, P], bf16)
        idx_src = sb("idx_src", [P, U, 2 * J], i32)
        mid_i, mid_row = sb("mid_i", [2, 1], i32), sb("mid_row", [2, 2 * F])
        feat = sb("feat", [P, NT, 4 * F])
        feat_f = feat[:, :, :].rearrange("p w c -> p (w c)")
        arena = sb("arena", [P, 2 * U * 2 * BLK])
        gat = arena[:, 0:U * 2 * BLK].rearrange("p (u j h c) -> p u j h c", u=U, j=J, h=2)
        seed = arena[:, U * 2 * BLK:2 * U * 2 * BLK].rearrange("p (u h j c) -> p u h j c", u=U, j=J, h=2)
        zbuf = arena[:, 0:U * 2 * BLK].rearrange("p (u n) -> p u n", u=U)
        ebuf = arena[:, U * 2 * BLK:2 * U * 2 * BLK].rearrange("p (u n) -> p u n", u=U)
        gat1 = arena[:, :].rearrange("p (u m) -> p u m", u=U)[:, :, 0:2 * J * F]
        attr = sb("attr", [P, 2, 2 * J * P])
        keep = sb("keep", [P, 2, 2 * BLK], bf16)
        neg, pos = sb("neg", [P, 2, 2 * BLK], bf16), sb("pos", [P, 2, 2 * BLK], bf16)
        res = sb("res", [P, 2, 3, BLK + 1])
        dif, expd = sb("dif", [P, 2, 2 * BLK]), sb("expd", [P, 2, 2 * BLK])
        eT = dif
        totals = feat_f[:, 0:U * 2 * BLK].rearrange("p (u n) -> p u n", u=U)
        msg = dif[:, :, :].rearrange("p a (b n) -> p (a b) n", n=BLK)
        mex = sb("mex", [P, BLK])
        hot_lo = pos[:, :, :].rearrange("p s (n c) -> p s n c", c=P)
        hot_hi = sb("hot_hi", [P, 2, 2 * J, NT], bf16)
        obuf = sb("obuf", [P, 2, 2 * J * 3 * F])
        obuf_f = obuf[:, :, :].rearrange("p s n -> p (s n)")
        xres, tab = sb("xres", [P, NT, F]), sb("tab", [P, NT, F])
        tmp, tmp2 = (arena[:, n * NT * F:(n + 1) * NT * F].rearrange("p (w c) -> p w c", c=F) for n in range(2))
        row0 = sb("row0", [P, 3 * F])
        cnt, pre, endf, flag, full, dinv, amp, mu, var = (
            sb(n, [P, NT]) for n in ("cnt", "pre", "endf", "flag", "full", "dinv", "amp", "mu", "var"))
        endi, starti = sb("endi", [P, NT], i32), sb("starti", [P, NT], i32)
        deglo, deghi = sb("deglo", [P, NT]), sb("deghi", [P, NT])
        aT = expd
        stats = feat[:, :, :].rearrange("p w c -> p (w c)")[:, 0:2 * NB * 6].rearrange("p (n k) -> p n k", k=6)
        agg2 = sb("agg2", [P, 2])
        bnsc, bnbi = sb("bnsc", [P, 2]), sb("bnbi", [P, 2])
        nrow = sb("nrow", [P, 4, F])
        col1 = sb("col1", [P, 4])
        w0T = sb("w0T", [F, F])
        w1s, w2s = sb("w1s", [F, F]), sb("w2s", [F, F])
        wdT, wsT, weT = sb("wdT", [F, P]), sb("wsT", [F, P]), sb("weT", [P, P])
        wtop, wbot = sb("wtop", [F, 2, F]), sb("wbot", [F, 2, F])
        weS, weST = sb("weS", [16, 2, F]), sb("weST", [F, 2, 16])
        cS = sb("cS", [16, 2, F])
        wblk = sb("wblk", [P, 2, J, P])
        wpost = obuf_f[:, 0:512].rearrange("p (l n c) -> p l n c", l=2, n=4)
        wpostT = obuf_f[0:F, 512:1536].rearrange("p (l n c) -> p l n c", l=2, n=4)
        wlin = sb("wlin", [F, 2, F])
        wcomb = sb("wcomb", [P, 2, 2, 2 * F])
        vecs = sb("vecs", [F, 2, 2])
        vecb = obuf_f[0:F, 1536:2048].rearrange("p (l n c) -> p l n c", l=2, n=2)
        fcraw, wraw0 = obuf_f[:, 2048:2304], obuf_f[0:F, 2304:2304 + F]
        B = {n: sb("B" + n, [P, k * F]) for n, k in (
            ("b0", 1), ("b1", 1), ("b2", 1), ("fcb", 2), ("bn2w", 1), ("bn2b", 1), ("bpre", 2),
            ("blin", 2), ("gamma", 2), ("beta", 2))}
        bnw_c, bnb_c = sb("bnw_c", [P, 2]), sb("bnb_c", [P, 2])

        pm = pb("pm", [P, 2, BLK])
        pt = pb("pt", [P, 3, BLK])
        pe_ = pb("pe_", [P, 2, BLK])
        ph = pb("ph", [P, BLK])

        one = lambda ps, k=1: {p: k for p in ps}
        ring = lambda name, adds: Ring(sem, name, adds)
        s_idx = ring("s_idx", one(GATHER))
        s_gat = ring("s_gat", one(GATHER, 2 * J * 16))
        s_att = ring("s_att", {SOFT: 32, STAT: 32, MSG: 32, PNA1: 32, PNA2: 32})
        s_kee = ring("s_kee", one((*SCANS, STAT), 32))
        s_neg = ring("s_neg", one((SOFT, *PNA)))
        s_eT = ring("s_eT", one((STAT, *PNA)))
        s_eC = ring("s_eC", one((STAT, *PNA)))
        s_col = ring("s_col", one(GATHER))
        s_zero_out = ring("s_zero_out", one((GCN1, GCN2), 16))
        s_sed = ring("s_sed", one((STAT,), 32))
        s_seT = ring("s_seT", one((STAT,)))
        s_cus = ring("s_cus", one(GATHER))
        s_hot = ring("s_hot", one((SOFT,)))
        s_hus = ring("s_hus", one((SOFT,)))
        s_dif = ring("s_dif", one((SOFT,)))
        s_exp = ring("s_exp", one((SOFT,)))
        s_abs = ring("s_abs", one((MSG,)))
        s_e1 = ring("s_e1", one((MSG,)))
        s_ln = ring("s_ln", one((MSG,)))
        s_sp = ring("s_sp", one((MSG,)))
        s_sg = ring("s_sg", one((MSG,)))
        s_res = ring("s_res", one((*SCANS, STAT)))
        s_row = ring("s_row", one(SCANS))
        s_rev = ring("s_rev", one(SCANS))
        s_out = ring("s_out", one((*SCANS, STAT), 16))
        s_lk = ring("s_lk", {SOFT: 3, MSG: 3, **one((GCN1, GCN2, STAT, *PNA), 0)})
        s_c, s_ld, s_w, s_wp, s_wc, s_wd = (sem(n) for n in ("s_c", "s_ld", "s_w", "s_wp", "s_wc", "s_wd"))
        s_kw, s_kd, s_dve, s_pre, s_zero = (sem(n) for n in ("s_kw", "s_kd", "s_dve", "s_pre", "s_zero"))
        s_h, s_cum, s_cnt, s_end, s_endg, s_r0, s_free = (sem(n) for n in (
            "s_h", "s_cum", "s_cnt", "s_end", "s_endg", "s_r0", "s_free"))
        s_oh, s_ohm = sem("s_oh"), sem("s_ohm")
        s_a2s, s_a2d = sem("s_a2s"), sem("s_a2d")
        s_p2s, s_p2d = sem("s_p2s"), sem("s_p2d")
        s_in, s_tr, s_tc, s_mm, s_po = (sem(n) for n in ("s_in", "s_tr", "s_tc", "s_mm", "s_po"))
        s_tb, s_td, s_fin, s_t1, s_bn, s_mi, s_mid, s_sc, s_at0 = (sem(n) for n in (
            "s_tb", "s_td", "s_fin", "s_t1", "s_bn", "s_mi", "s_mid", "s_sc", "s_at0"))
        s_go = sem("s_go")
        block = ctx.enter_context(nc.Block())

        def feats(w, c):
            return feat[:, w, c * P:(c + 1) * P]
        ENDS = (SOFT, GCN1, GCN2, MSG, PNA1, PNA2)
        CALLS = [
            (lambda w, c: tmp[:, w, :], F, 1, lambda c: w0T[:, :], F),
            (lambda w, c: xres[:, w, :], F, 1, lambda c: w1s[:, :], F),
            (lambda w, c: tmp[:, w, :], F, 1, lambda c: w2s[:, :], F),
            (lambda w, c: xres[:, w, :], F, 1, lambda c: wsT[:, :], 2 * F),
            (lambda w, c: xres[:, w, :], F, 1, lambda c: wdT[:, :], 2 * F),
            (lambda w, c: xres[:, w, :], F, 1, lambda c: wtop[:, 0, :], F),
            (feats, P, 2, lambda c: wcomb[:, 0, c, :], 2 * F),
            (lambda w, c: feat[:, w, 0:F], F, 1, lambda c: wtop[:, 1, :], F),
            (feats, P, 2, lambda c: wcomb[:, 1, c, :], 2 * F),
        ]
        STEPS = [(k, g, c) for k, call in enumerate(CALLS) for g in range(NG) for c in range(call[2])]
        first_step = {k: next(n for n, s in enumerate(STEPS) if s[0] == k) for k in range(len(CALLS))}

        calls_before = {SOFT: 0, GCN1: 2, GCN2: 3, STAT: 5, MSG: 5, PNA1: 6, PNA2: 8}
        LOADED = 16 * (4 + 2 * 10 + 6 + 4 + 8 + 2)
        TABLE = {GCN1: 16, GCN2: 32, STAT: 64, PNA1: 80, PNA2: 96}
        SKIP = OVER % BLK
        assert OVER // BLK == 1
        wide = feat[:, :, :].rearrange("p w c -> p (w c)").bitcast(i32)
        EW = 2 * H // P
        cur_i, prev_i, src_i, dst_i, lo_i, hi_i = (wide[:, n * EW:(n + 1) * EW] for n in range(6))
        as_blocks = lambda a: a.rearrange("p (h b j) -> p h b j", h=2, j=J)
        flat = lambda a: a[:, :, :, :].rearrange("p h b j -> p (h b j)")
        keep_w = hot_lo[:, :, :, :].rearrange("p s n c -> p (s n c)")[:, 0:EW]
        blk = lambda i, u: i * U + u

        @block.sync
        def _(sp):
            nload = 0

            def load(o, i):
                nonlocal nload
                sp.dma_start(o, i).then_inc(s_ld, 16)
                nload += 1

            for h, e0 in ((0, 0), (1, BASE1)):
                for to, of in ((dst_i, dst), (src_i, src)):
                    sp.dma_start(as_blocks(to)[:, h, :, :], of[e0:e0 + H].rearrange("(b p j) -> p b j", p=P, j=J))\
                      .then_inc(s_pre, 16)
            half = H // P
            for h, e0 in ((0, 0), (1, BASE1)):
                sp.dma_start(cur_i[:, h * half:(h + 1) * half], dst[e0:e0 + H].rearrange("(p n) -> p n", p=P)).then_inc(s_pre, 16)
            sp.dma_start(prev_i[:, half:2 * half], dst[BASE1 - 1:E - 1].rearrange("(p n) -> p n", p=P)).then_inc(s_pre, 16)
            sp.dma_start(prev_i[1:P, 0:half], dst[half - 1:H - 1].rearrange("(p n) -> p n", n=half)).then_inc(s_pre, 16)
            sp.dma_start(prev_i[0:1, 1:half], dst[0:half - 1].rearrange("(a n) -> a n", a=1)).then_inc(s_pre, 16)
            load(wraw0[:, :], W0)
            load(w1s[:, :], W1)
            load(w2s[:, :], W2)
            load(fcraw[:, :], fcw)
            for l in range(2):
                load(wtop[:, l, :], Wpre[l, 0:F, :])
                load(wbot[:, l, :], Wpre[l, F:2 * F, :])
                load(weS[:, l, :], We[l, :, :])
                load(wlin[:, l, :], Wlin[l, :, :])
                load(wpost[:, l, 0, :], Wpost[l, 0:P, :])
                load(wpost[:, l, 1, :], Wpost[l, P:2 * P, :])
                load(wpost[F:P, l, 2, :], Wpost[l, 2 * P:2 * P + F, :])
                load(wpost[:, l, 3, :], Wpost[l, 2 * P + F:3 * P + F, :])
                load(vecs[:, l, 0:1], be[l, :].rearrange("(c a) -> c a", a=1))
                load(vecs[:, l, 1:2], bpost[l, :].rearrange("(c a) -> c a", a=1))
            for n, v in (("b0", b0), ("b1", b1), ("b2", b2), ("fcb", fcb), ("bn2w", bn2w), ("bn2b", bn2b)):
                load(B[n][:, :], v.rearrange("(a c) -> a c", a=1).broadcast_to([P, v.shape[0]]))
            for n, v in (("bpre", bpre), ("blin", blin), ("gamma", gamma), ("beta", beta)):
                load(B[n][:, :], v.rearrange("(a l) c -> a (l c)", a=1).broadcast_to([P, 2 * F]))
            for part in range(2):
                for h in range(2):
                    at = slice(h * F, h * F + F)
                    load(bnw_c[at, part:part + 1], bn1w[part * F:part * F + F].rearrange("(c a) -> c a", a=1))
                    load(bnb_c[at, part:part + 1], bn1b[part * F:part * F + F].rearrange("(c a) -> c a", a=1))
            sp.wait_ge(s_zero, 1)
            load(xres[:, 0:NT - 1, :], x[0:(NT - 1) * P, :].rearrange("(w p) c -> p w c", p=P))
            load(xres[0:LAST, NT - 1, :], x[(NT - 1) * P:N, :])
            assert nload * 16 == LOADED

            sp.wait_ge(s_wc, 1)
            for l in range(2):
                for j in range(J):
                    for h in range(2):
                        r = h * F + j * 16
                        sp.dma_start(wblk[r:r + 16, l, j, h * F:h * F + F], cS[:, l, :]).then_inc(s_wd, 16)
            sp.dma_start(mid_i[:, :], dst[H:H + 1].rearrange("(a n) -> a n", a=1).broadcast_to([2, 1])).then_inc(s_mi, 16)
            sp.wait_ge(s_kw, 1)
            for h in range(2):
                sp.dma_start(keep_d[h, :].rearrange("(p n) -> p n", p=P), keep_w[:, h * half:(h + 1) * half]).then_inc(s_kd, 16)
            sp.wait_ge(s_kd, 32)

            def attr_load(p, i, u):
                b = blk(i, u)
                if p == MSG and u % 2 == 0:
                    s_abs.done(sp, p, i, u, back=U - 1)
                    for h in range(2):
                        for part in range(2):
                            sp.dma_start(totals[h * F:h * F + F, u:u + 2, part * BLK:(part + 1) * BLK],
                                         total_d[bass.ds(b, 2), part * F:part * F + F, h, :]
                                         .rearrange("a c n -> c a n")).then_inc(s_att.sems[u + part], 16)
                if p not in (SOFT, STAT, *PNA):
                    return
                s_col.done(sp, p, i, u, back=2)
                for h, e0 in ((0, 0), (1, BASE1)):
                    rows = bass.ds(b * BLK + e0, BLK)
                    if p == SOFT:
                        to = attr[:, u % 2, 0:2 * J * F].rearrange("p (j h c) -> p j h c", j=J, h=2)[:, :, h, :]
                        of = ea64[rows, :].rearrange("(p j) c -> p j c", j=J)
                    elif p == STAT:
                        to = attr[:, u % 2, h * J * P:(h + 1) * J * P]
                        of = ea128[rows, :].rearrange("(p j) c -> p (j c)", j=J)
                    elif p in PNA:
                        to = attr[:, u % 2, h * F:h * F + F]
                        of = ea16[rows, :].rearrange("(p j) c -> p (j c)", j=J)
                    sp.dma_start(to, of).then_inc(s_att.sems[u], 16)

            def seed_work(p, i, u):
                b = blk(i, u)
                if p in (GCN1, GCN2):
                    r0 = (0, H)[p == GCN2]
                    sp.dma_start(seed_d[bass.ds(b * BLK + r0, BLK), :].rearrange("(p j) c -> p (j c)", j=J),
                                 attr[:, 0, 0:J * 2 * F]).then_inc(s_zero_out.sems[u], 16)
                elif p == STAT:
                    s_seT.done(sp, p, i, u, back=U)
                    for h in range(2):
                        sp.dma_start(seed[:, u, h, :, :].rearrange("p j c -> p (j c)"),
                                     seed_d[bass.ds(b * BLK + h * H, BLK), :].rearrange("(p j) c -> p (j c)", j=J))\
                          .then_inc(s_sed.sems[u], 16)

            def mask_load(p, i, u):
                if u % 2:
                    return
                s_res.done(sp, p, i, u, back=U - 1)
                if p == STAT:
                    for h, to in enumerate((keep, neg)):
                        sp.dma_start(to[:, u // 2, :],
                                     keep_d[h:h + 1, bass.ds(blk(i, u) * BLK, 2 * BLK)].broadcast_to([P, 2 * BLK]))\
                          .then_inc(s_kee.sems[u], 16)
                    return
                for h in range(2):
                    sp.dma_start(keep[h * F:h * F + F, u // 2, :],
                                 keep_d[h:h + 1, bass.ds(blk(i, u) * BLK, 2 * BLK)].broadcast_to([F, 2 * BLK]))\
                      .then_inc(s_kee.sems[u], 16)

            ntab = 0
            for p in range(7):
                if p == GCN1:
                    sp.wait_ge(s_at0, 1)
                if p == STAT:
                    s_zero_out.all_done(sp, GCN2)
                    sp.wait_ge(s_td, 16 * 4)
                    sp.wait_ge(s_mid, 16)
                    sp.wait_ge(s_sc, 16 * NT)
                    sp.dma_start(seed_d[H + OVER:H + OVER + 1, :], mid_row[0:1, :]).then_inc(s_mi, 16)
                    sp.wait_ge(s_mi, 32)
                if p == MSG:
                    s_out.all_done(sp, STAT)
                    sp.wait_ge(s_wc, 3)
                for u in range(U):
                    mask_load(p, 0, u)
                    seed_work(p, 0, u)
                    attr_load(p, 0, u)
                with sp.Fori(1, IT) as i:
                    for u in range(U):
                        if p == MSG:
                            attr_load(p, i, u)
                            mask_load(p, i, u)
                        else:
                            mask_load(p, i, u)
                            seed_work(p, i, u)
                            attr_load(p, i, u)
                if p == STAT:
                    s_out.all_done(sp, STAT)
                    sp.dma_start(eT[:, 0, 0:BLK - SKIP], total_d[OVER // BLK, :, 1, SKIP:BLK]).then_inc(s_t1, 16)
                    continue
                s_out.all_done(sp, p)
                r, k = (runs3_d, 3) if UNITS[p] == 3 else (runs1_d, 1)
                if p > 0:
                    sp.wait_ge(s_free, ENDS.index(p))
                sp.dma_start(row0[:, 0:k * F], r[H - 1:H, :].broadcast_to([P, k * F])).then_inc(s_r0, 16)
                if p == GCN2:
                    sp.wait_ge(s_tb, 3)
                    sp.dma_start(tsrc_d.rearrange("(w p) c -> p w c", p=P), feat[:, :, 0:2 * F]).then_inc(s_td, 16)
                    sp.wait_ge(s_tb, 4)
                    sp.dma_start(tdst_d.rearrange("(w p) c -> p w c", p=P), feat[:, :, 2 * F:4 * F]).then_inc(s_td, 16)
                elif p != PNA2:
                    n = {SOFT: 0, GCN1: 1, MSG: 2, PNA1: 3}[p]
                    sp.wait_ge(s_tb, {0: 1, 1: 2, 2: 5, 3: 6}[n])
                    sp.dma_start(table_d[n].rearrange("(w p) c -> p w c", p=P), tab[:, :, :]).then_inc(s_td, 16)
            sp.wait_ge(s_tb, 7)
            sp.dma_start(out[0:(NT - 1) * P, :].rearrange("(w p) c -> p w c", p=P), tab[:, 0:NT - 1, :]).then_inc(s_fin, 16)
            sp.dma_start(out[(NT - 1) * P:N, :], tab[0:LAST, NT - 1, :]).then_inc(s_fin, 16)
            sp.wait_ge(s_fin, 32)

        @block.gpsimd
        def _(g):
            g.memset(ident[:, :], 1.0).then_inc(s_c, 1)
            g.memset(tri[:, :], 1.0).then_inc(s_c, 1)
            g.memset(ones[:, :], 1.0).then_inc(s_c, 1)
            g.memset(onesN[:, :], 1.0 / N).then_inc(s_c, 1)
            g.memset(valid[:, :], 1.0).then_inc(s_c, 1)
            g.iota(iota[:, :], pattern=[[1, P]], base=0, channel_multiplier=0,
                   allow_small_or_imprecise_dtypes=True).then_inc(s_c, 1)
            g.wait_ge(s_c, 6)
            g.affine_select(out=ident[:, :], in_=ident[:, :], compare_op=ALU.is_equal, fill=0.0, base=0,
                            pattern=[[-1, P]], channel_multiplier=1).then_inc(s_c, 1)
            g.affine_select(out=tri[:, :], in_=tri[:, :], compare_op=ALU.is_ge, fill=0.0, base=0,
                            pattern=[[1, P]], channel_multiplier=-1).then_inc(s_c, 1)
            g.affine_select(out=valid[:, :], in_=valid[:, :], compare_op=ALU.is_ge, fill=0.0, base=LAST - 1,
                            pattern=[[0, 1]], channel_multiplier=-1).then_inc(s_c, 1)

            def rows(p, i, u):
                s_idx.done(g, p, i, u)
                s_col.done(g, p, i, u, back=U)
                g.sem_inc(s_go, 1)
                table = {SOFT: x, GCN1: table_d[0], GCN2: table_d[1], STAT: tsrc_d,
                         PNA1: table_d[2], PNA2: table_d[3]}[p]
                for h in range(2):
                    for j in range(J):
                        to = gat[:, u, j, h, :] if p == STAT else gat1[:, u, (j * 2 + h) * F:(j * 2 + h + 1) * F]
                        idx = idx_src[:, u, h * J + j:h * J + j + 1]
                        g.indirect_dma_start(out=to, out_offset=None, in_=table,
                                             in_offset=bass.IndirectOffsetOnAxis(ap=idx, axis=0))\
                         .then_inc(s_gat.sems[u], 16)

            nend = 0
            for p in range(7):
                if p != MSG:
                    if p != SOFT:
                        g.wait_ge(s_td, TABLE[p])
                    if p == STAT:
                        g.wait_ge(s_mi, 16)
                        g.indirect_dma_start(out=mid_row[:, :], out_offset=None, in_=tdst_d,
                                             in_offset=bass.IndirectOffsetOnAxis(ap=mid_i[:, 0:1], axis=0)).then_inc(s_mid, 16)
                        for q in (GCN1, GCN2):
                            s_zero_out.all_done(g, q)
                        for w in range(NT):
                            g.indirect_dma_start(out=seed_d, out_offset=bass.IndirectOffsetOnAxis(ap=starti[:, w:w + 1], axis=0),
                                                 in_=feat[:, w, 2 * F:4 * F], in_offset=None,
                                                 bounds_check=2 * H - 1, oob_is_err=False).then_inc(s_sc, 16)
                    for u in range(U):
                        rows(p, 0, u)
                    with g.Fori(1, IT) as i:
                        for u in range(U):
                            rows(p, i, u)
                if p == STAT:
                    continue
                g.wait_ge(s_end, 1)
                s_out.all_done(g, p)
                if p > 0:
                    g.wait_ge(s_free, ENDS.index(p))
                r, k = (runs3_d, 3) if UNITS[p] == 3 else (runs1_d, 1)
                for w in range(NT):
                    g.indirect_dma_start(out=feat[:, w, F:F + k * F], out_offset=None, in_=r,
                                         in_offset=bass.IndirectOffsetOnAxis(ap=endi[:, w:w + 1], axis=0))\
                     .then_inc(s_endg, 16)

        @block.tensor
        def _(pe):
            mm = nc.tensor.matmul
            pe.wait_ge(s_c, 9)
            pe.wait_ge(s_ld, LOADED)
            def tp(o, i, k):
                return nc.tensor.transpose(o, i, ident[0:k, 0:k])
            pe.wait_ge(s_wp, 1)
            tp(pm[0:F, 0, 0:F], wraw0[:, :], F)
            tp(pm[0:F, 0, F:F + P], fcraw[:, 0:F], P)
            tp(pm[0:F, 0, F + P:F + 2 * P], fcraw[:, F:2 * F], P)
            for l in range(2):
                tp(pm[0:F, 0, 2 * P + F + 16 * l:2 * P + F + 16 * l + 16], weS[:, l, :], 16)
            tp(pm[:, 1, 0:P], fcraw[:, 2 * F:4 * F], P)
            for l in range(2):
                for c in range(4):
                    last = tp(pt[0:F, l, c * P:(c + 1) * P], wpost[:, l, c, :], P)
            last.then_inc(s_w, 1)
            pe.wait_ge(s_wp, 2)
            for l in range(2):
                for c in range(4):
                    mm(pe_[:, l, c * F:(c + 1) * F], wpostT[:, l, c, :], wlin[:, l, :], start=True, stop=True)
                mm(pe_[:, l, 4 * F:5 * F], vecb[:, l, 1, :], wlin[:, l, :], start=True, stop=True)
                mm(pe_[:, l, 5 * F:6 * F], vecb[:, l, 0, :], wbot[:, l, :], start=True, stop=True)
                last = mm(pe_[0:16, l, 6 * F:7 * F], weST[:, l, :], wbot[:, l, :], start=True, stop=True)
            last.then_inc(s_w, 1)
            pe.wait_ge(s_wc, 1)
            pe.wait_ge(s_wd, 16 * 16)

            def turn_features(p, i, u):
                if p not in (STAT, *PNA):
                    return
                s_att.done(pe, p, i, u)
                s_eC.done(pe, p, i, u, back=1)
                if p == STAT:
                    for h in range(2):
                        for j in range(J):
                            last = nc.tensor.transpose(pe_[:, h, j:BLK:J], attr[:, u % 2, (h * J + j) * P:(h * J + j + 1) * P], ident[:, :])
                else:
                    last = nc.tensor.transpose(pe_[:, 0, 0:P], attr[:, u % 2, 0:P], ident[:, :])
                last.then_inc(s_eT.sems[u], 1)

            def columns(p, i, u):
                if p == MSG:
                    return
                s = u % 2
                s_gat.done(pe, p, i, u)
                s_cus.done(pe, p, i, u, back=2)
                if p == SOFT:
                    s_att.done(pe, p, i, u)
                if p in (STAT, *PNA):
                    s_eC.done(pe, p, i, u)
                if p == STAT:
                    for h in range(2):
                        to = (pm[:, h, :], pt[:, 1 + h, :])[s]
                        mm(to, weT[:, :], eT[:, s, h * BLK:(h + 1) * BLK], start=True, stop=False, skip_group_check=True)
                        for j in range(J):
                            last = mm(to[:, j:BLK:J], gat[:, u, j, h, :], ident[:, :],
                                      start=False, stop=True, skip_group_check=True)
                else:
                    for j in range(J):
                        to = pm[:, s, j:BLK:J]
                        if p == SOFT:
                            mm(to, attr[:, u % 2, j * P:(j + 1) * P], ident[:, :], start=True, stop=False, skip_group_check=True)
                        if p in PNA:
                            mm(to, wblk[:, PNA.index(p), j, :], eT[:, s, 0:P], start=True, stop=False, skip_group_check=True)
                        last = mm(to, gat1[:, u, j * P:(j + 1) * P], ident[:, :],
                                  start=(p in (GCN1, GCN2)), stop=True, skip_group_check=True)
                last.then_inc(s_col.sems[u], 1)

            def turn_seeds(p, i, u):
                if p != STAT:
                    return
                s_sed.done(pe, p, i, u)
                s_res.done(pe, p, i, u, back=1)
                for h in range(2):
                    for j in range(J):
                        last = nc.tensor.transpose((pt[:, 0, :], ph[:, :])[h][:, j:BLK:J], seed[:, u, h, j, :], ident[:, :])
                last.then_inc(s_seT.sems[u], 1)

            def turn_back(p, i, u):
                if p == SOFT:
                    s_hot.done(pe, p, i, u)
                    for n in range(2 * J):
                        last = mm(ph[:, 0:NT], hot_lo[:, u % 2, n, :], hot_hi[:, u % 2, n, :],
                                  start=False, stop=False, skip_group_check=True)
                    last.then_inc(s_hus.sems[u], 1)
                if p == STAT:
                    return
                s_res.done(pe, p, i, u)
                s_rev.done(pe, p, i, u, back=1)
                for k in range(UNITS[p]):
                    for j in range(J):
                        last = nc.tensor.transpose(pt[:, k, j * P:(j + 1) * P], res[:, u % 2, k, 1 + j:1 + BLK:J], ident[:, :])
                last.then_inc(s_row.sems[u], 1)

            small = 0

            def small_product(n, o, w, v):
                pe.wait_ge(s_p2s, n)
                mm(o, w, v, start=True, stop=True).then_inc(s_p2d, 1)

            def node_matmuls(calls):
                steps = [n for n, s in enumerate(STEPS) if s[0] in calls]

                def turn(n):
                    k, gr, c = STEPS[n]
                    rows_, width = CALLS[k][0], CALLS[k][1]
                    if n == first_step[k]:
                        pe.wait_ge(s_in, k + 1)
                    if n >= 2:
                        pe.wait_ge(s_tc, n - 1)
                    a, z = GROUPS[gr]
                    for w in range(a, z):
                        last = nc.tensor.transpose(pe_[0:width, n % 2, (w - a) * P:(w - a + 1) * P], rows_(w, c), ident[:, :])
                    last.then_inc(s_tr, 1)

                def product(n):
                    k, gr, c = STEPS[n]
                    _, width, chunks, weight, cols = CALLS[k]
                    G = k * NG + gr
                    pe.wait_ge(s_tc, n + 1)
                    if c == 0 and G >= 2:
                        pe.wait_ge(s_po, G - 1)
                    a, z = GROUPS[gr]
                    for w in range(a, z):
                        last = mm(pm[:, G % 2, (w - a) * cols:(w - a + 1) * cols], aT[0:width, n % 2, (w - a) * P:(w - a + 1) * P],
                                  weight(c), start=(c == 0 and w == a), stop=(c == chunks - 1), skip_group_check=True)
                    last.then_inc(s_mm, 1)

                turn(steps[0])
                for n in steps:
                    if n + 1 <= steps[-1] and STEPS[n + 1][0] == STEPS[n][0]:
                        turn(n + 1)
                        product(n)
                    else:
                        product(n)
                        if n + 1 <= steps[-1]:
                            turn(n + 1)

            for p in range(7):
                if p == SOFT:
                    pe.wait_ge(s_wc, 2)
                    mm(ph[:, 0:NT], hot_lo[:, 1, 0, :], hot_hi[:, 1, 0, :], start=True, stop=False, skip_group_check=True).then_inc(s_h, 1)
                if p != SOFT:
                    pe.wait_ge(s_po, calls_before[p] * NG)
                turn_features(p, 0, 0)
                columns(p, 0, 0)
                turn_features(p, 0, 1)
                turn_seeds(p, 0, 0)

                def body(i, end):
                    for u in range(U):
                        nxt, nx2 = (i + (u + 1) // U, (u + 1) % U), (i + (u + 2) // U, (u + 2) % U)
                        if not (end and u + 1 >= U):
                            columns(p, *nxt)
                        if not (end and u + 2 >= U):
                            turn_features(p, *nx2)
                        if not (end and u + 1 >= U):
                            turn_seeds(p, *nxt)
                        turn_back(p, i, u)

                body(0, False)
                with pe.Fori(1, IT - 1) as i:
                    body(i, False)
                body(IT - 1, True)
                if p == SOFT:
                    pe.wait_ge(s_zero, 2)
                    mm(ph[:, 0:NT], hot_lo[:, 0, 0, :], hot_hi[:, 0, 0, :], start=False, stop=True, skip_group_check=True).then_inc(s_h, 1)
                    pe.wait_ge(s_cnt, 1)
                    mm(ph[:, 64:64 + NT], tri[:, :], cnt[:, :], start=True, stop=True)
                    mm(ph[:, 128:128 + NT], ones[:, :], cnt[:, :], start=True, stop=True).then_inc(s_cum, 1)
                    for w in range(NT):
                        pe.wait_ge(s_oh, w + 1)
                        mm(ph[:, 256:256 + NT], hot_lo[:, w % 2, 0, :], hot_hi[:, w % 2, 0, :],
                           start=(w == 0), stop=(w == NT - 1), skip_group_check=True).then_inc(s_ohm, 1)
                    small_product(1, ph[:, 384:385], ones[:, :], col1[:, 0:1])
                    node_matmuls([0])
                    node_matmuls([1])
                elif p == GCN1:
                    node_matmuls([2])
                elif p == GCN2:
                    node_matmuls([3])
                    node_matmuls([4])
                elif p == STAT:
                    pe.wait_ge(s_p2s, 2)
                    for h in range(2):
                        for part in range(2):
                            last = mm(ph[h * F:h * F + F, 2 * part:2 * part + 2], ident[:, part * F:part * F + F], agg2[:, :],
                                      start=True, stop=True)
                    last.then_inc(s_bn, 1)
                elif p == MSG:
                    small_product(3, ph[:, 0:F], onesN[:, :], nrow[:, 0, :])
                    small_product(4, ph[:, F:2 * F], onesN[:, :], nrow[:, 1, :])
                    node_matmuls([5])
                elif p == PNA1:
                    node_matmuls([6])
                    small_product(5, ph[:, 0:F], onesN[:, :], nrow[:, 0, :])
                    small_product(6, ph[:, F:2 * F], onesN[:, :], nrow[:, 1, :])
                    node_matmuls([7])
                elif p == PNA2:
                    node_matmuls([8])
                    small_product(7, ph[:, 0:F], onesN[:, :], nrow[:, 0, :])
                    small_product(8, ph[:, F:2 * F], onesN[:, :], nrow[:, 1, :])

        @block.scalar
        def _(act):
            A = nc.scalar.activation

            def masks(p, i, u):
                if p not in (SOFT, *PNA) or u % 2:
                    return
                v = u // 2
                s_kee.done(act, p, i, u)
                s_res.done(act, p, i, u, back=U - 1)
                if p in PNA:
                    A(pos[:, v, :], keep[:, v, :], ACT.Copy, scale=-BIG, bias=BIG)
                A(neg[:, v, :], keep[:, v, :], ACT.Copy, scale=BIG, bias=-BIG).then_inc(s_neg.sems[u], 1)

            def rows_out(p, i, u):
                s_row.done(act, p, i, u)
                s_out.done(act, p, i, u, back=2)
                K, s = UNITS[p], u % 2
                to = obuf[:, s, 0:2 * J * K * F]
                for k in range(K):
                    last = A(to.rearrange("p (h j k c) -> p k j h c", h=2, j=J, k=K)[:, k, :, :, :],
                             pt[:, k, :].rearrange("p (j h c) -> p j h c", j=J, h=2), ACT.Copy)
                last.then_inc(s_rev.sems[u], 1)
                s_rev.done(act, p, i, u)
                r = runs3_d if K == 3 else runs1_d
                act.dma_start(r.rearrange("(h n) c -> h n c", h=2)[:, bass.ds(blk(i, u) * BLK, BLK), :]
                              .rearrange("h (p j) c -> p h (j c)", j=J),
                              to.rearrange("p (h q) -> p h q", h=2)).then_inc(s_out.sems[u], 16)

            def features(p, i, u):
                s_eT.done(act, p, i, u)
                s_col.done(act, p, i, u, back=2)
                s = u % 2
                if p == STAT:
                    A(eT[:, s, :], pe_[:, :, :].rearrange("p h n -> p (h n)"), ACT.Copy).then_inc(s_eC.sems[u], 1)
                else:
                    A(eT[:, s, 0:P], pe_[:, 0, 0:P], ACT.Copy).then_inc(s_eC.sems[u], 1)

            def logs(i, u):
                s_abs.done(act, MSG, i, u)
                A(ebuf[:, u, :], ebuf[:, u, :], ACT.Exp, scale=-1.0).then_inc(s_e1.sems[u], 1)
                s_e1.done(act, MSG, i, u)
                A(ebuf[:, u, :], ebuf[:, u, :], ACT.Ln, bias=1.0).then_inc(s_ln.sems[u], 1)

            def gate(i, u):
                s_sp.done(act, MSG, i, u)
                A(zbuf[:, u, 0:BLK], zbuf[:, u, 0:BLK], ACT.Exp).then_inc(s_sg.sems[u], 1)

            def body(p, i, end):
                for u in range(U):
                    nxt, nx2 = (i + (u + 1) // U, (u + 1) % U), (i + (u + 2) // U, (u + 2) % U)
                    if p in (STAT, *PNA) and not (end and u + 2 >= U):
                        features(p, *nx2)
                    masks(p, i, u)
                    s = u % 2
                    if p == SOFT:
                        s_dif.done(act, p, i, u)
                        A(expd[:, s, :], dif[:, s, :], ACT.Exp).then_inc(s_exp.sems[u], 1)
                    if p == STAT:
                        s_cus.done(act, p, i, u)
                        act.dma_start(total_d[bass.ds(blk(i, u), 1), :, :, :].rearrange("a p h n -> (a p) (h n)"),
                                      expd[:, s, :]).then_inc(s_out.sems[u], 16)
                        continue
                    if p == MSG:
                        if not (end and u + 2 >= U):
                            logs(*nx2)
                        if not (end and u + 1 >= U):
                            gate(*nxt)
                        if u > 0:
                            rows_out(p, i, u - 1)
                        elif not (isinstance(i, int) and i == 0):
                            rows_out(p, i - 1, U - 1)
                        continue
                    rows_out(p, i, u)

            def node_copies(calls):
                for n, (k, gr, c) in enumerate(STEPS):
                    if k not in calls:
                        continue
                    act.wait_ge(s_tr, n + 1)
                    if n >= 2:
                        act.wait_ge(s_mm, n - 1)
                    width, cols = CALLS[k][1], (GROUPS[gr][1] - GROUPS[gr][0]) * P
                    A(aT[0:width, n % 2, 0:cols], pe_[0:width, n % 2, 0:cols], ACT.Copy).then_inc(s_tc, 1)

            asked = 0

            def small(o, i, f, **kw):
                nonlocal asked
                asked += 1
                act.wait_ge(s_a2s, asked)
                A(o, i, f, **kw).then_inc(s_a2d, 1)

            act.wait_ge(s_wc, 1)
            for p in range(7):
                if p in (STAT, *PNA):
                    features(p, 0, 0)
                    features(p, 0, 1)
                if p == MSG:
                    small(col1[:, 2:4], col1[:, 0:2], ACT.Sqrt)
                    act.wait_ge(s_wc, 3)
                    act.preload_act_table_set("natural_log_exp_and_others")
                    logs(0, 0)
                    logs(0, 1)
                    gate(0, 0)
                body(p, 0, False)
                with act.Fori(1, IT - 1) as i:
                    body(p, i, False)
                body(p, IT - 1, True)
                if p == MSG:
                    rows_out(p, IT - 1, U - 1)
                if p == SOFT:
                    small(dinv[:, :], mu[:, :], ACT.Sqrt)
                    small(amp[:, :], mu[:, :], ACT.Ln)
                    small(mu[:, :], var[:, :], ACT.Ln, bias=1.0)
                    small(tmp[:, :, :], tmp[:, :, :], ACT.Exp)
                    small(tmp2[:, :, :], tmp2[:, :, :], ACT.Exp)
                    node_copies([0])
                    small(var[:, :], var[:, :], ACT.Sqrt)
                    node_copies([1])
                elif p == GCN1:
                    node_copies([2])
                elif p == GCN2:
                    small(var[:, :], var[:, :], ACT.Sqrt)
                    node_copies([3, 4])
                elif p == MSG:
                    small(nrow[:, 2, :], nrow[:, 2, :], ACT.Sqrt)
                    small(tmp2[:, :, :], tmp2[:, :, :], ACT.Exp)
                    small(tmp2[:, :, :], tmp2[:, :, :], ACT.Ln, bias=1.0)
                    small(var[:, :], var[:, :], ACT.Sqrt)
                    node_copies([5])
                elif p == PNA1:
                    node_copies([6])
                    small(nrow[:, 2, :], nrow[:, 2, :], ACT.Sqrt)
                    node_copies([7])
                elif p == PNA2:
                    node_copies([8])
                    small(nrow[:, 2, :], nrow[:, 2, :], ACT.Sqrt)
                    small(var[:, :], var[:, :], ACT.Sqrt)

        @block.vector
        def _(dve):
            V = nc.vector
            TT, TS, STT, SCAN = V.tensor_tensor, V.tensor_scalar, V.scalar_tensor_tensor, V.tensor_tensor_scan
            chain = 0

            def link(ins):
                nonlocal chain
                chain += 1
                ins.then_inc(s_dve, 1)
                dve.wait_ge(s_dve, chain)

            asked = [0, 0]

            def ask_scalar():
                asked[0] += 1
                dve.sem_inc(s_a2s, 1)
                dve.wait_ge(s_a2d, asked[0])

            def ask_tensor():
                asked[1] += 1
                dve.sem_inc(s_p2s, 1)
                dve.wait_ge(s_p2d, asked[1])

            link(V.memset(xres[:, NT - 1, :], 0.0))
            dve.sem_inc(s_zero, 1)
            link(V.memset(wpost[0:F, :, 2, :], 0.0))
            link(V.memset(wblk[:, :, :, :], 0.0))
            dve.wait_ge(s_ld, LOADED)
            link(V.tensor_copy(vecb[:, :, :, :], vecs[:, :, :].unsqueeze(3).broadcast_to([F, 2, 2, P])))
            dve.sem_inc(s_wp, 1)

            dve.wait_ge(s_pre, 9 * 16)
            link(V.memset(prev_i[0:1, 0:1], 0))
            link(TT(keep_w, cur_i, prev_i, ALU.is_equal))
            link(V.memset(keep_w[0:1, 0:1], 0.0))
            link(V.memset(keep_w[0:1, H // P:H // P + 1], 0.0))
            link(V.memset(keep_w[0:1, H // P + OVER:H // P + OVER + 1], 0.0))
            dve.sem_inc(s_kw, 1)

            def copy_indices(p, i, u, new):
                b = new
                last = TS(idx_src[:, u, :].rearrange("p (h j) -> p h j", h=2), src_all[:, :, bass.ds(b, 1), :].rearrange("p h a j -> p h (a j)"), 0.0, None, ALU.add)
                last.then_inc(s_idx.sems[u], 1)

            link(V.tensor_copy(flat(src_all), src_i))
            for u in range(U):
                copy_indices(SOFT, 0, u, u)
            link(TS(lo_i, dst_i, P - 1, None, ALU.bitwise_and))
            link(TS(hi_i, dst_i, 7, None, ALU.logical_shift_right))
            link(V.tensor_copy(flat(dlo), lo_i))
            link(V.tensor_copy(flat(dhi), hi_i))
            link(V.memset(dhi[:, 1, 0:1, :], float(P)))
            link(V.memset(dhi[0:SKIP // J, 1, 1:2, :], float(P)))

            dve.wait_ge(s_w, 1)
            link(V.tensor_copy(w0T[:, :], pm[0:F, 0, 0:F]))
            link(V.tensor_copy(wdT[:, :], pm[0:F, 0, F:F + P]))
            link(V.tensor_copy(wsT[:, :], pm[0:F, 0, F + P:F + 2 * P]))
            link(V.tensor_copy(weST[:, :, :].rearrange("c l k -> c (l k)"), pm[0:F, 0, 2 * P + F:2 * P + F + 32]))
            link(V.tensor_copy(weT[:, :], pm[:, 1, 0:P]))
            for l in range(2):
                link(V.tensor_copy(wpostT[:, l, :, :].rearrange("c n q -> c (n q)"), pt[0:F, l, :]))
            dve.sem_inc(s_wp, 1)
            dve.wait_ge(s_w, 2)
            for l in range(2):
                for c in range(2):
                    for k in range(2):
                        link(V.tensor_copy(wcomb[:, l, c, k * F:(k + 1) * F], pe_[:, l, (2 * k + c) * F:(2 * k + c + 1) * F]))
                v = slice(l * F, l * F + F)
                link(TT(B["blin"][:, v], pe_[:, l, 4 * F:5 * F], B["blin"][:, v], ALU.add))
                link(TT(B["bpre"][:, v], pe_[:, l, 5 * F:6 * F], B["bpre"][:, v], ALU.add))
                link(V.tensor_copy(cS[:, l, :], pe_[0:16, l, 6 * F:7 * F]))
            dve.sem_inc(s_wc, 1)
            dve.wait_ge(s_kd, 32)
            for s in range(2):
                link(V.memset(hot_lo[:, s, 0, :], 0.0))
                link(V.memset(hot_hi[:, s, 0, :], 0.0))
            dve.sem_inc(s_wc, 1)
            dve.wait_ge(s_h, 1)

            def scan(p, u, k, mask, data, mul=False, low=False):
                s = u % 2
                return SCAN(res[:, s, k, 1:BLK + 1], mask, data, res[:, 1 - s, k, BLK:BLK + 1],
                            ALU.mult if mul else ALU.add, ALU.add if mul else ALU.min if low else ALU.max)

            def chained_on(p, i, u, n, ins):
                ins.then_inc(s_lk.sems[u], 1)
                dve.wait_ge(s_lk.sems[u], i * s_lk.adds[p] + (s_lk.base[p] + n))

            def scaled(i, u):
                s_att.done(dve, MSG, i, u - u % 2)
                s_att.done(dve, MSG, i, u - u % 2 + 1)
                TS(zbuf[:, u, 0:BLK], totals[:, u, 0:BLK], bnsc[:, 0:1], bnbi[:, 0:1], ALU.mult, ALU.add)
                chained_on(MSG, i, u, 1, TS(zbuf[:, u, BLK:], totals[:, u, BLK:2 * BLK], bnsc[:, 1:2], bnbi[:, 1:2],
                                            ALU.mult, ALU.add))
                TS(ebuf[:, u, :].bitcast(i32), zbuf[:, u, :].bitcast(i32), 0x7fffffff, None, ALU.bitwise_and).then_inc(s_abs.sems[u], 1)

            def softplus(i, u):
                s_ln.done(dve, MSG, i, u)
                STT(zbuf[:, u, 0:BLK], zbuf[:, u, 0:BLK], 0.0, ebuf[:, u, 0:BLK], ALU.min, ALU.subtract).then_inc(s_sp.sems[u], 1)
                chained_on(MSG, i, u, 2, STT(msg[:, u, :], zbuf[:, u, BLK:], 0.0, ebuf[:, u, BLK:], ALU.max, ALU.add))

            def step(p, i, u, end):
                s, v, half = u % 2, u // 2, slice((u % 2) * BLK, (u % 2) * BLK + BLK)
                nlink = 0 if p != MSG else 2

                def chained(ins):
                    nonlocal nlink
                    nlink += 1
                    chained_on(p, i, u, nlink, ins)

                if p in GATHER:
                    s_col.done(dve, p, i, u)
                    if not end:
                        copy_indices(p, i, u, i * U + (u + U))
                if p == MSG:
                    if not (end and u + 2 >= U):
                        scaled(i + (u + 2) // U, (u + 2) % U)
                    if not (end and u + 1 >= U):
                        softplus(i + (u + 1) // U, (u + 1) % U)
                if p in SCANS:
                    s_row.done(dve, p, i, u, back=2)
                    s_res.done(dve, p, i, u, back=1)
                if p in (SOFT, *PNA):
                    s_neg.done(dve, p, i, u - u % 2)
                else:
                    s_kee.done(dve, p, i, u - u % 2)
                col = pm[:, s, :]
                if p in (GCN1, GCN2):
                    last = scan(p, u, 0, keep[:, v, half], col, mul=True)
                    last.then_inc(s_res.sems[u], 1)
                    s_res.done(dve, p, i, u)
                    dve.sem_inc(s_cus.sems[u], 1)
                elif p in PNA:
                    scan(p, u, 0, keep[:, v, half], col, mul=True)
                    scan(p, u, 1, pos[:, v, half], col, low=True)
                    scan(p, u, 2, neg[:, v, half], col).then_inc(s_res.sems[u], 1)
                    s_res.done(dve, p, i, u)
                    dve.sem_inc(s_cus.sems[u], 1)
                elif p == SOFT:
                    V.tensor_copy(res[:, s, 0, 0:1], res[:, 1 - s, 0, BLK:BLK + 1])
                    chained(scan(p, u, 0, neg[:, v, half], col))
                    R = res[:, s, 0, 1:BLK + 1]
                    chained(TT(dif[:, s, 0:BLK], res[:, s, 0, 0:BLK], neg[:, v, half], ALU.add))
                    TT(dif[:, s, BLK:], col, R, ALU.subtract)
                    TT(dif[:, s, 0:BLK], dif[:, s, 0:BLK], R, ALU.subtract).then_inc(s_dif.sems[u], 1)
                    s_hus.done(dve, p, i, u, back=2)
                    for hot, part, n in ((hot_lo, dlo, P), (hot_hi, dhi, NT)):
                        last = TT(hot[:, s, :, :].rearrange("p (h j) c -> p h j c", h=2),
                                  part[:, :, bass.ds(i * U + u, 1), :].rearrange("p h a j -> p h (a j)").unsqueeze(3).broadcast_to([P, 2, J, n]),
                                  iota[:, 0:n].unsqueeze(1).unsqueeze(1).broadcast_to([P, 2, J, n]), ALU.is_equal)
                    last.then_inc(s_hot.sems[u], 1)
                    s_exp.done(dve, p, i, u)
                    chained(TT(mex[:, :], col, expd[:, s, BLK:], ALU.mult))
                    dve.sem_inc(s_cus.sems[u], 1)
                    scan(p, u, 1, expd[:, s, 0:BLK], expd[:, s, BLK:], mul=True)
                    scan(p, u, 2, expd[:, s, 0:BLK], mex[:, :], mul=True).then_inc(s_res.sems[u], 1)
                    s_res.done(dve, p, i, u)
                elif p == STAT:
                    s_res.done(dve, p, i, u, back=1)
                    s_seT.done(dve, p, i, u)
                    for h in range(2):
                        last = scan(p, u, h, (keep, neg)[h][:, v, half], (pt[:, 0, :], ph[:, :])[h], mul=True)
                    last.then_inc(s_res.sems[u], 1)
                    s_out.done(dve, p, i, u, back=2)
                    s_res.done(dve, p, i, u)
                    for h in range(2):
                        last = TT(expd[:, s, h * BLK:(h + 1) * BLK], (pm[:, h, :], pt[:, 1 + h, :])[s], res[:, s, h, 1:BLK + 1], ALU.add)
                    last.then_inc(s_cus.sems[u], 1)
                    s_cus.done(dve, p, i, u)
                    for h in range(2):
                        V.bn_stats(stats[:, bass.ds(i * U + (u + h * NB), 1), :].rearrange("p a k -> p (a k)"),
                                   expd[:, s, h * BLK:(h + 1) * BLK])
                elif p == MSG:
                    s_sg.done(dve, p, i, u)
                    chained(TT(msg[:, u, :], msg[:, u, :], zbuf[:, u, 0:BLK], ALU.mult))
                    scan(p, u, 0, keep[:, v, half], msg[:, u, :], mul=True).then_inc(s_res.sems[u], 1)

            def edge_pass(p):
                link(V.memset(res[:, 1, :, BLK:BLK + 1], 0.0))
                if p in GATHER and p != SOFT:
                    for u in range(U):
                        copy_indices(p, 0, u, u)
                if p == MSG:
                    scaled(0, 0)
                    scaled(0, 1)
                    softplus(0, 0)
                for u in range(U):
                    step(p, 0, u, False)
                with dve.Fori(1, IT - 1) as i:
                    for u in range(U):
                        step(p, i, u, False)
                for u in range(U):
                    step(p, IT - 1, u, True)

            over_f = lambda a: a.unsqueeze(2).broadcast_to([P, NT, F])
            over_w = lambda a, n=NT: a.unsqueeze(1).broadcast_to([P, n, F])
            by_f = lambda a: a.rearrange("p w c -> p c w")
            part = lambda k: feat[:, :, k * F:(k + 1) * F]

            def keep_valid(a):
                link(TS(a[:, NT - 1, :], a[:, NT - 1, :], valid[:, 0:1], None, ALU.mult))

            def layer_norm(a, t, o):
                link(V.reduce_sum(mu[:, :], a, axis=AX.X))
                link(TS(mu[:, :], mu[:, :], 1.0 / F, None, ALU.mult))
                link(TT(a, a, over_f(mu[:, :]), ALU.subtract))
                link(TT(t, a, a, ALU.mult))
                link(V.reduce_sum(var[:, :], t, axis=AX.X))
                link(TS(var[:, :], var[:, :], 1.0 / F, 1e-5, ALU.mult, ALU.add))
                ask_scalar()
                link(V.reciprocal(var[:, :], var[:, :]))
                link(TT(o, a, over_f(var[:, :]), ALU.mult))

            def batch_norm(a, t, w, b):
                keep_valid(a)
                link(V.reduce_sum(nrow[:, 0, :], by_f(a), axis=AX.X))
                ask_tensor()
                link(V.tensor_copy(nrow[:, 3, :], ph[:, 0:F]))
                link(TT(t, a, over_w(nrow[:, 3, :]), ALU.subtract))
                keep_valid(t)
                link(TT(a, t, t, ALU.mult))
                link(V.reduce_sum(nrow[:, 1, :], by_f(a), axis=AX.X))
                ask_tensor()
                link(TS(nrow[:, 2, :], ph[:, F:2 * F], 1e-5, None, ALU.add))
                ask_scalar()
                link(V.reciprocal(nrow[:, 3, :], nrow[:, 2, :]))
                link(TT(nrow[:, 3, :], nrow[:, 3, :], w, ALU.mult))
                link(TT(a, t, over_w(nrow[:, 3, :]), ALU.mult))
                link(TT(a, a, over_w(b), ALU.add))

            def node_call(k, post):
                dve.sem_inc(s_in, 1)
                cols = CALLS[k][4]
                nstep = [n for n, s in enumerate(STEPS) if s[0] == k]
                for g, (a, z) in enumerate(GROUPS):
                    last = nstep[0] + (g + 1) * CALLS[k][2]
                    dve.wait_ge(s_mm, last)
                    G = k * NG + g
                    post(a, z, pm[:, G % 2, 0:(z - a) * cols].rearrange("p (n c) -> p n c", c=cols)).then_inc(s_po, 1)
                dve.wait_ge(s_po, (k + 1) * NG)

            def ends(p):
                n = ENDS.index(p) + 1
                dve.wait_ge(s_endg, n * NT * 16)
                dve.wait_ge(s_r0, n * 16)

            def whole_sum(k):
                link(TT(tmp[:, :, :], over_w(row0[:, 0:F]), over_f(flag[:, :]), ALU.mult))
                link(TT(part(k), part(k), tmp[:, :, :], ALU.add))
                link(TT(part(k), part(k), over_f(full[:, :]), ALU.mult))

            def table_free(p):
                if p in TABLE:
                    dve.wait_ge(s_td, TABLE[p])

            def counts():
                dve.wait_ge(s_hus.sems[U - 1], s_hus.base[SOFT] + IT)
                link(V.memset(hot_lo[:, 0, 0, :], 0.0))
                link(V.memset(hot_hi[:, 0, 0, :], 0.0))
                dve.sem_inc(s_zero, 1)
                dve.wait_ge(s_h, 2)
                link(V.tensor_copy(cnt[:, :], ph[:, 0:NT]))
                dve.sem_inc(s_cnt, 1)
                dve.wait_ge(s_cum, 1)
                link(V.tensor_copy(pre[:, :], ph[:, 128:128 + NT]))
                link(SCAN(var[:, :], ones[:, 0:NT], pre[:, :], 0.0, ALU.mult, ALU.add))
                link(TT(var[:, :], var[:, :], pre[:, :], ALU.subtract))
                link(TT(endf[:, :], ph[:, 64:64 + NT], var[:, :], ALU.add))
                link(TT(pre[:, :], endf[:, :], cnt[:, :], ALU.subtract))
                link(TS(mu[:, :], pre[:, :], float(H), None, ALU.is_ge))
                link(STT(deghi[:, :], mu[:, :], float(OVER), pre[:, :], ALU.mult, ALU.add))
                link(TS(endf[:, :], endf[:, :], 1.0, 0.0, ALU.subtract, ALU.max))
                link(TS(var[:, :], endf[:, :], float(H), None, ALU.is_ge))
                link(TS(pre[:, :], pre[:, :], float(H), None, ALU.is_lt))
                link(TS(full[:, :], cnt[:, :], 0.0, None, ALU.is_gt))
                link(TT(flag[:, :], pre[:, :], var[:, :], ALU.mult))
                link(TT(flag[:, :], flag[:, :], full[:, :], ALU.mult))
                link(STT(endf[:, :], var[:, :], float(OVER), endf[:, :], ALU.mult, ALU.add))
                link(V.tensor_copy(endi[:, :], endf[:, :]))
                link(TS(mu[:, :], full[:, :], -2.0 ** 20, 2.0 ** 20, ALU.mult, ALU.add))
                link(TT(mu[:, :], mu[:, :], deghi[:, :], ALU.add))
                link(V.tensor_copy(starti[:, :], mu[:, :]))
                dve.sem_inc(s_end, 1)
                link(TS(mu[:, :], cnt[:, :], 1.0, None, ALU.add))
                ask_scalar()
                link(V.reciprocal(dinv[:, :], dinv[:, :]))
                link(TS(mu[:, :], cnt[:, :], 1.0, 1.0, ALU.max, ALU.add))
                ask_scalar()
                i0, i1 = mu[:, :].bitcast(i32), var[:, :].bitcast(i32)
                link(V.tensor_copy(i0, cnt[:, :]))
                link(TS(i1, i0, P - 1, None, ALU.bitwise_and))
                link(V.tensor_copy(deglo[:, :], i1))
                link(TS(i1, i0, 7, None, ALU.logical_shift_right))
                link(V.tensor_copy(deghi[:, :], i1))
                link(TS(col1[:, 0:1], valid[:, 0:1], -1000.0, 1000.0, ALU.mult, ALU.add))
                link(TT(deghi[:, NT - 1:NT], deghi[:, NT - 1:NT], col1[:, 0:1], ALU.add))
                for w in range(NT):
                    if w >= 2:
                        dve.wait_ge(s_ohm, w - 1)
                    link(TS(hot_lo[:, w % 2, 0, :], iota[:, :], deglo[:, w:w + 1], None, ALU.is_equal))
                    TS(hot_hi[:, w % 2, 0, :], iota[:, 0:NT], deghi[:, w:w + 1], None, ALU.is_equal).then_inc(s_oh, 1)
                dve.wait_ge(s_ohm, NT)
                link(V.tensor_copy(var[:, :], ph[:, 256:256 + NT]))
                ask_scalar()
                link(TT(mu[:, NT - 1:NT], mu[:, NT - 1:NT], valid[:, 0:1], ALU.mult))
                link(V.reduce_sum(col1[:, 0:1], mu[:, :], axis=AX.X))
                ask_tensor()
                link(TS(col1[:, 1:2], ph[:, 384:385], 1.0 / N, None, ALU.mult))
                link(V.reciprocal(col1[:, 1:2], col1[:, 1:2]))
                link(TS(amp[:, :], amp[:, :], col1[:, 1:2], None, ALU.mult))

            def extreme(k, op, sign):
                link(TS(mu[:, :], flag[:, :], 1.0, sign * BIG, ALU.subtract, ALU.mult))
                link(TT(tmp[:, :, :], over_w(row0[:, (k - 1) * F:k * F]), over_f(flag[:, :]), ALU.mult))
                link(TT(tmp[:, :, :], tmp[:, :, :], over_f(mu[:, :]), ALU.add))

            T, T2 = tmp[:, :, :], tmp2[:, :, :]
            X, TAB = xres[:, :, :], tab[:, :, :]

            edge_pass(SOFT)
            link(V.memset(attr[:, :, :], 0.0))
            dve.sem_inc(s_at0, 1)
            counts()
            ends(SOFT)
            extreme(1, ALU.max, 1.0)
            link(TT(TAB, part(1), T, ALU.max))
            link(TT(T2, part(1), TAB, ALU.subtract))
            link(TT(T, T, TAB, ALU.subtract))
            ask_scalar()
            ask_scalar()
            for k in (2, 3):
                link(TT(part(k), part(k), T2, ALU.mult))
                link(TT(TAB, over_w(row0[:, (k - 1) * F:k * F]), T, ALU.mult))
                link(TT(part(k), part(k), TAB, ALU.add))
            link(TS(part(2), part(2), 1e-38, None, ALU.max))
            link(V.reciprocal(T2, part(2)))
            link(TT(T, part(3), T2, ALU.mult))
            link(TT(T, T, over_f(full[:, :]), ALU.mult))
            node_call(0, lambda a, z, o: TT(tmp2[:, a:z, :], o, over_w(B["b0"][:, :], z - a), ALU.add))
            link(STT(T2, T2, 0.0, X, ALU.max, ALU.add))
            link(TT(T2, T2, X, ALU.add))
            layer_norm(T2, T, X)
            by_dinv = lambda a, z, o: TT(tab[:, a:z, :], o, dinv[:, a:z].unsqueeze(2).broadcast_to([P, z - a, F]), ALU.mult)
            node_call(1, by_dinv)
            dve.sem_inc(s_tb, 1)
            dve.sem_inc(s_free, 1)

            for p in (GCN1, GCN2):
                edge_pass(p)
                ends(p)
                table_free(p)
                whole_sum(1)
                link(TT(T, part(1), TAB, ALU.add))
                link(TT(T, T, over_f(dinv[:, :]), ALU.mult))
                link(TT(T, T, over_w(B["b1" if p == GCN1 else "b2"][:, :]), ALU.add))
                if p == GCN1:
                    link(TS(T, T, 0.0, None, ALU.max))
                    node_call(2, by_dinv)
                    dve.sem_inc(s_tb, 1)
                else:
                    link(TT(T, T, X, ALU.add))
                    layer_norm(T, T2, X)
                    node_call(3, lambda a, z, o: V.tensor_copy(feat[:, a:z, 0:2 * F], o))
                    dve.sem_inc(s_tb, 1)
                    node_call(4, lambda a, z, o: TT(feat[:, a:z, 2 * F:4 * F], o,
                                                    B["fcb"][:, :].unsqueeze(1).broadcast_to([P, z - a, 2 * F]), ALU.add))
                    dve.sem_inc(s_tb, 1)
                dve.sem_inc(s_free, 1)

            edge_pass(STAT)
            dve.wait_ge(s_t1, 16)
            link(V.bn_stats(stats[:, NB + 1, :], eT[:, 0, 0:BLK - SKIP]))
            link(V.tensor_copy(stats[:, NB, :], stats[:, 2 * NB - 1, :]))
            link(V.bn_aggr(agg2[:, :], stats[:, 0:2 * NB - 1, :].rearrange("p n k -> p (n k)")))
            dve.sem_inc(s_p2s, 1)
            dve.wait_ge(s_bn, 1)
            link(V.tensor_copy(nrow[:, 0, 0:4], ph[:, 0:4]))
            link(TS(col1[:, 0:2], nrow[:, 0, 1:4:2], 1e-5, None, ALU.add))
            ask_scalar()
            link(V.reciprocal(col1[:, 2:4], col1[:, 2:4]))
            link(TT(bnsc[:, :], bnw_c[:, :], col1[:, 2:4], ALU.mult))
            link(TT(bnbi[:, :], bnsc[:, :], nrow[:, 0, 0:4:2], ALU.mult))
            link(TT(bnbi[:, :], bnb_c[:, :], bnbi[:, :], ALU.subtract))
            dve.sem_inc(s_wc, 1)

            edge_pass(MSG)
            ends(MSG)
            whole_sum(1)
            link(V.tensor_copy(T, part(1)))
            batch_norm(T, T2, B["bn2w"][:, :], B["bn2b"][:, :])
            link(TT(T, T, X, ALU.add))
            link(STT(T2, T, -1.0, T, ALU.mult, ALU.min))
            ask_scalar()
            ask_scalar()
            link(STT(T, T, 0.0, T2, ALU.max, ALU.add))
            link(TT(T, T, X, ALU.add))
            layer_norm(T, T2, X)
            node_call(5, lambda a, z, o: TT(tab[:, a:z, :], o, over_w(B["bpre"][:, 0:F], z - a), ALU.add))
            dve.sem_inc(s_tb, 1)
            link(V.tensor_copy(part(0), X))
            dve.sem_inc(s_free, 1)

            for l, p in enumerate(PNA):
                v = slice(l * F, l * F + F)
                edge_pass(p)
                ends(p)
                table_free(p)
                whole_sum(1)
                link(TS(mu[:, :], cnt[:, :], 1.0, None, ALU.max))
                link(V.reciprocal(mu[:, :], mu[:, :]))
                link(TT(part(1), part(1), over_f(mu[:, :]), ALU.mult))
                for k, op, sign in ((2, ALU.min, -1.0), (3, ALU.max, 1.0)):
                    extreme(k, op, sign)
                    link(TT(part(k), part(k), T, op))
                    link(TT(part(k), part(k), over_f(full[:, :]), ALU.mult))

                def post(a, z, o):
                    link(TT(tmp[:, a:z, :], o[:, :, F:2 * F], amp[:, a:z].unsqueeze(2).broadcast_to([P, z - a, F]), ALU.mult))
                    return TT(tmp[:, a:z, :], tmp[:, a:z, :], o[:, :, 0:F], ALU.add)

                node_call(6 if l == 0 else 8, post)
                link(TT(T, T, over_w(B["blin"][:, v]), ALU.add))
                batch_norm(T, T2, B["gamma"][:, v], B["beta"][:, v])
                link(TS(T, T, 0.0, None, ALU.max))
                if l == 0:
                    link(V.tensor_copy(part(0), T))
                    node_call(7, lambda a, z, o: TT(tab[:, a:z, :], o, over_w(B["bpre"][:, F:2 * F], z - a), ALU.add))
                    dve.sem_inc(s_tb, 1)
                    dve.sem_inc(s_free, 1)
                else:
                    link(TT(T, T, X, ALU.add))
                    layer_norm(T, T2, TAB)
                    dve.sem_inc(s_tb, 1)


_INS = ["x", "src", "dst", "edge_attr_128", "edge_attr_16", "edge_attr_64", "L0_gnn_W", "L0_gnn_b",
        "L1_gnn_W1", "L1_gnn_b1", "L1_gnn_W2", "L1_gnn_b2", "L2_gnn_fc_w", "L2_gnn_fc_b",
        "L2_gnn_bn1_w", "L2_gnn_bn1_b", "L2_gnn_bn2_w", "L2_gnn_bn2_b", "L3_gnn_We", "L3_gnn_be",
        "L3_gnn_Wpre", "L3_gnn_bpre", "L3_gnn_Wpost", "L3_gnn_bpost", "L3_gnn_Wlin", "L3_gnn_blin",
        "L3_gnn_gamma", "L3_gnn_beta"]


def kernel(**inputs):
    import numpy as _np
    import concourse.bacc as _bacc
    from concourse import mybir as _mybir
    from concourse.bass_utils import run_bass_kernel_spmd as _run

    nc = _bacc.Bacc("TRN2", target_bir_lowering=False, num_devices=1)
    arrays, args = {}, []
    for name in _INS:
        a = _np.ascontiguousarray(inputs[name])
        arrays[f"in_{name}_dram"] = a
        args.append(nc.dram_tensor(f"in_{name}_dram", a.shape, _mybir.dt.from_np(a.dtype), kind="ExternalInput").ap())
    args.append(nc.dram_tensor("out_0_dram", (6250, 64), _mybir.dt.float32, kind="ExternalOutput").ap())
    gnn_kernel(nc, *args)
    r = _run(nc, [arrays], core_ids=[0])
    return r.results[0]["out_0_dram"]
```

```python
import concourse.bass as bass
from concourse import mybir
from contextlib import ExitStack

N, E, F = 6250, 200000, 64
P = 128
NT = -(-N // P)
NP = NT * P
LAST = N - (NT - 1) * P
J = 4
BLK = P * J
U = 4
NB = -(-(-(-(E // 2) // BLK)) // U) * U
H = NB * BLK
IT = NB // U
BASE1 = E - H
OVER = H - BASE1
BIG = 3e38
SOFT, GCN1, GCN2, STAT, MSG, PNA1, PNA2 = range(7)
GATHER = (SOFT, GCN1, GCN2, STAT, PNA1, PNA2)
SCANS = (SOFT, GCN1, GCN2, MSG, PNA1, PNA2)
PNA = (PNA1, PNA2)
UNITS = {SOFT: 3, GCN1: 1, GCN2: 1, MSG: 1, PNA1: 3, PNA2: 3}
GS = 4
GROUPS = [(a, min(a + GS, NT)) for a in range(0, NT, GS)]
PARTS = [(0, 3), (3, 6), (6, 9), (9, len(GROUPS))]
Q = len(PARTS)
SPAN = [(GROUPS[a][0], GROUPS[z - 1][1]) for a, z in PARTS]


class Ring:

    def __init__(self, sem, name, adds):
        self.sems = [sem(f"{name}{u}") for u in range(U)]
        self.adds, self.base, total = adds, {}, 0
        for p in range(7):
            self.base[p] = total
            total += adds.get(p, 0) * IT

    def done(self, engine, p, i, u, back=0):
        own = u >= back
        value = i * self.adds[p] + (self.base[p] + self.adds[p] * own)
        if not (isinstance(value, int) and value <= 0):
            engine.wait_ge(self.sems[u - back if own else u - back + U], value)

    def all_done(self, engine, p):
        for u in range(U):
            engine.wait_ge(self.sems[u], self.base[p] + IT * self.adds[p])


def gnn_kernel(nc, x, src, dst, ea128, ea16, ea64, W0, b0, W1, b1, W2, b2, fcw, fcb, bn1w, bn1b,
               bn2w, bn2b, We, be, Wpre, bpre, Wpost, bpost, Wlin, blin, gamma, beta, out):
    f32, bf16, i32, u16 = mybir.dt.float32, mybir.dt.bfloat16, mybir.dt.int32, mybir.dt.uint16
    ALU, ACT, AX = mybir.AluOpType, mybir.ActivationFunctionType, mybir.AxisListType
    dram = lambda name, shape, dt=f32: nc.dram_tensor(name, shape, dt, kind="Internal").ap()
    keep_d = dram("keep_d", (2, H), bf16)
    table_d = [dram(f"table_d{p}", (NP, F)) for p in range(4)]
    tsrc_d, tdst_d = dram("tsrc_d", (NP, 2 * F)), dram("tdst_d", (NP, 2 * F))
    runs1_d, runs3_d = dram("runs1_d", (2 * H, F)), dram("runs3_d", (2 * H, 3 * F))
    seed_d = dram("seed_d", (2 * H, 2 * F))
    total_d = dram("total_d", (NB, P, 2, BLK))

    ctx = ExitStack()
    with ctx:
        sb = lambda name, shape, dt=f32: ctx.enter_context(nc.sbuf_tensor(name, shape, dt))
        pb = lambda name, shape, dt=f32: ctx.enter_context(nc.psum_tensor(name, shape, dt))
        sem = lambda name: ctx.enter_context(nc.semaphore(name))

        ident, onesN = sb("ident", [P, P]), sb("onesN", [P, P])
        tri, ones = sb("tri", [P, P]), sb("ones", [P, P])
        valid = sb("valid", [P, 1])
        src_all = sb("src_all", [P, 2, NB, J], u16)
        dlo, dhi = sb("dlo", [P, 2, NB, J], bf16), sb("dhi", [P, 2, NB, J], bf16)
        iota = sb("iota", [P, P], bf16)
        idx_src = sb("idx_src", [P, U, 2 * J], i32)
        mid_i, mid_row = sb("mid_i", [2, 1], i32), sb("mid_row", [2, 2 * F])
        feat = sb("feat", [P, NT, 4 * F])
        feat_f = feat[:, :, :].rearrange("p w c -> p (w c)")
        arena = sb("arena", [P, 2 * U * 2 * BLK])
        gat = arena[:, 0:U * 2 * BLK].rearrange("p (u j h c) -> p u j h c", u=U, j=J, h=2)
        seed = arena[:, U * 2 * BLK:2 * U * 2 * BLK].rearrange("p (u h j c) -> p u h j c", u=U, j=J, h=2)
        zbuf = arena[:, 0:U * 2 * BLK].rearrange("p (u n) -> p u n", u=U)
        ebuf = arena[:, U * 2 * BLK:2 * U * 2 * BLK].rearrange("p (u n) -> p u n", u=U)
        gat1 = arena[:, :].rearrange("p (u m) -> p u m", u=U)[:, :, 0:2 * J * F]
        attr = sb("attr", [P, 2, 2 * J * P])
        keep = sb("keep", [P, 2, 2 * BLK], bf16)
        neg, pos = sb("neg", [P, 2, 2 * BLK], bf16), sb("pos", [P, 2, 2 * BLK], bf16)
        res = sb("res", [P, 2, 3, BLK + 1])
        dif, expd = sb("dif", [P, 2, 2 * BLK]), sb("expd", [P, 2, 2 * BLK])
        eT = dif
        totals = feat_f[:, 0:U * 2 * BLK].rearrange("p (u n) -> p u n", u=U)
        msg = dif[:, :, :].rearrange("p a (b n) -> p (a b) n", n=BLK)
        mex = sb("mex", [P, BLK])
        hot_lo = pos[:, :, :].rearrange("p s (n c) -> p s n c", c=P)
        hot_hi = sb("hot_hi", [P, 2, 2 * J, NT], bf16)
        obuf = sb("obuf", [P, 2, 2 * J * 3 * F])
        obuf_f = obuf[:, :, :].rearrange("p s n -> p (s n)")
        xres, tab = sb("xres", [P, NT, F]), sb("tab", [P, NT, F])
        tmp, tmp2 = (arena[:, n * NT * F:(n + 1) * NT * F].rearrange("p (w c) -> p w c", c=F) for n in range(2))
        row0 = sb("row0", [P, 3 * F])
        cnt, pre, endf, flag, full, dinv, amp, mu, var = (
            sb(n, [P, NT]) for n in ("cnt", "pre", "endf", "flag", "full", "dinv", "amp", "mu", "var"))
        endi, starti = sb("endi", [P, NT], i32), sb("starti", [P, NT], i32)
        deglo, deghi = sb("deglo", [P, NT]), sb("deghi", [P, NT])
        aT = expd
        stats = feat[:, :, :].rearrange("p w c -> p (w c)")[:, 0:2 * NB * 6].rearrange("p (n k) -> p n k", k=6)
        agg2 = sb("agg2", [P, 2])
        bnsc, bnbi = sb("bnsc", [P, 2]), sb("bnbi", [P, 2])
        nrow = sb("nrow", [P, 4, F])
        col1 = sb("col1", [P, 4])
        w0T = sb("w0T", [F, F])
        w1s, w2s = sb("w1s", [F, F]), sb("w2s", [F, F])
        wdT, wsT, weT = sb("wdT", [F, P]), sb("wsT", [F, P]), sb("weT", [P, P])
        wtop, wbot = sb("wtop", [F, 2, F]), sb("wbot", [F, 2, F])
        weS, weST = sb("weS", [16, 2, F]), sb("weST", [F, 2, 16])
        cS = sb("cS", [16, 2, F])
        wblk = sb("wblk", [P, 2, J, P])
        wpost = obuf_f[:, 0:512].rearrange("p (l n c) -> p l n c", l=2, n=4)
        wpostT = obuf_f[0:F, 512:1536].rearrange("p (l n c) -> p l n c", l=2, n=4)
        wlin = sb("wlin", [F, 2, F])
        wcomb = sb("wcomb", [P, 2, 2, 2 * F])
        vecs = sb("vecs", [F, 2, 2])
        vecb = obuf_f[0:F, 1536:2048].rearrange("p (l n c) -> p l n c", l=2, n=2)
        fcraw, wraw0 = obuf_f[:, 2048:2304], obuf_f[0:F, 2304:2304 + F]
        B = {n: sb("B" + n, [P, k * F]) for n, k in (
            ("b0", 1), ("b1", 1), ("b2", 1), ("fcb", 2), ("bn2w", 1), ("bn2b", 1), ("bpre", 2),
            ("blin", 2), ("gamma", 2), ("beta", 2))}
        bnw_c, bnb_c = sb("bnw_c", [P, 2]), sb("bnb_c", [P, 2])

        pn = pb("pn", [P, 5, BLK])
        pm = pn[:, 0:2, :]
        pt = pn[:, 2:5, :]
        pe_ = pb("pe_", [P, 2, BLK])
        ph = pb("ph", [P, BLK])

        one = lambda ps, k=1: {p: k for p in ps}
        ring = lambda name, adds: Ring(sem, name, adds)
        s_idx = ring("s_idx", one(GATHER))
        s_gat = ring("s_gat", one(GATHER, 2 * J * 16))
        s_att = ring("s_att", {SOFT: 32, STAT: 32, MSG: 32, PNA1: 32, PNA2: 32})
        s_kee = ring("s_kee", one((*SCANS, STAT), 32))
        s_neg = ring("s_neg", one((SOFT, *PNA)))
        s_eT = ring("s_eT", one((STAT, *PNA)))
        s_eC = ring("s_eC", one((STAT, *PNA)))
        s_col = ring("s_col", one(GATHER))
        s_zero_out = ring("s_zero_out", one((GCN1, GCN2), 16))
        s_sed = ring("s_sed", one((STAT,), 32))
        s_seT = ring("s_seT", one((STAT,)))
        s_cus = ring("s_cus", one(GATHER))
        s_hot = ring("s_hot", one((SOFT,)))
        s_hus = ring("s_hus", one((SOFT,)))
        s_dif = ring("s_dif", one((SOFT,)))
        s_exp = ring("s_exp", one((SOFT,)))
        s_abs = ring("s_abs", one((MSG,)))
        s_e1 = ring("s_e1", one((MSG,)))
        s_ln = ring("s_ln", one((MSG,)))
        s_sp = ring("s_sp", one((MSG,)))
        s_sg = ring("s_sg", one((MSG,)))
        s_res = ring("s_res", one((*SCANS, STAT)))
        s_row = ring("s_row", one(SCANS))
        s_rev = ring("s_rev", one(SCANS))
        s_out = ring("s_out", one((*SCANS, STAT), 16))
        s_lk = ring("s_lk", {SOFT: 3, MSG: 3, **one((GCN1, GCN2, STAT, *PNA), 0)})
        s_c, s_ld, s_w, s_wp, s_wc, s_wd = (sem(n) for n in ("s_c", "s_ld", "s_w", "s_wp", "s_wc", "s_wd"))
        s_kw, s_kd, s_dve, s_pre, s_zero = (sem(n) for n in ("s_kw", "s_kd", "s_dve", "s_pre", "s_zero"))
        s_h, s_cum, s_cnt, s_end, s_r0, s_free = (sem(n) for n in (
            "s_h", "s_cum", "s_cnt", "s_end", "s_r0", "s_free"))
        s_endg = [sem(f"s_endg{q}") for q in range(Q)]
        s_oh, s_ohm = sem("s_oh"), sem("s_ohm")
        s_a2s, s_a2d = sem("s_a2s"), sem("s_a2d")
        s_p2s, s_p2d = sem("s_p2s"), sem("s_p2d")
        s_in, s_tr, s_tc, s_mm, s_po = (sem(n) for n in ("s_in", "s_tr", "s_tc", "s_mm", "s_po"))
        s_tb, s_td, s_t1, s_bn, s_mi, s_mid, s_sc, s_at0 = (sem(n) for n in (
            "s_tb", "s_td", "s_t1", "s_bn", "s_mi", "s_mid", "s_sc", "s_at0"))
        s_go = sem("s_go")
        block = ctx.enter_context(nc.Block())

        def feats(w, c):
            return feat[:, w, c * P:(c + 1) * P]
        ENDS = (SOFT, GCN1, GCN2, MSG, PNA1, PNA2)
        CALLS = [
            (lambda w, c: tmp[:, w, :], F, 1, lambda c: w0T[:, :], F),
            (lambda w, c: xres[:, w, :], F, 1, lambda c: w1s[:, :], F),
            (lambda w, c: tmp[:, w, :], F, 1, lambda c: w2s[:, :], F),
            (lambda w, c: xres[:, w, :], F, 1, lambda c: wsT[:, :], 2 * F),
            (lambda w, c: xres[:, w, :], F, 1, lambda c: wdT[:, :], 2 * F),
            (lambda w, c: xres[:, w, :], F, 1, lambda c: wtop[:, 0, :], F),
            (feats, P, 2, lambda c: wcomb[:, 0, c, :], 2 * F),
            (lambda w, c: feat[:, w, 0:F], F, 1, lambda c: wtop[:, 1, :], F),
            (feats, P, 2, lambda c: wcomb[:, 1, c, :], 2 * F),
        ]
        JOBS = []
        for calls, lags in (((0, 1), (0, 1)), ((2,), (0,)), ((3, 4), (0, 0)), ((5,), (0,)), ((6,), (0,)),
                            ((7,), (0,)), ((8,), (0,))):
            for t in range(Q + max(lags)):
                JOBS += [(k, t - lag) for k, lag in zip(calls, lags) if 0 <= t - lag < Q]
        STEPS = [(job, g, c) for job, (k, q) in enumerate(JOBS) for g in range(*PARTS[q]) for c in range(CALLS[k][2])]
        FILLS = [(job, g) for job, (k, q) in enumerate(JOBS) for g in range(*PARTS[q])]
        fill = {f: n for n, f in enumerate(FILLS)}
        step_of = {x: n for n, x in enumerate(STEPS)}
        job_of = {j: n for n, j in enumerate(JOBS)}
        of_calls = lambda *calls: [n for n, (k, q) in enumerate(JOBS) if k in calls]
        calls_before = {SOFT: 0, GCN1: 2, GCN2: 3, STAT: 5, MSG: 5, PNA1: 6, PNA2: 8}
        fills_before = {p: sum(JOBS[job][0] < n for job, _ in FILLS) for p, n in calls_before.items()}

        LOADED = 16 * (4 + 2 * 10 + 6 + 4 + 8 + 2)
        TABLE = {GCN1: 16 * Q, GCN2: 32 * Q, STAT: 64 * Q, PNA1: 80 * Q, PNA2: 96 * Q}
        SKIP = OVER % BLK
        assert OVER // BLK == 1
        wide = feat[:, :, :].rearrange("p w c -> p (w c)").bitcast(i32)
        EW = 2 * H // P
        cur_i, prev_i, src_i, dst_i, lo_i, hi_i = (wide[:, n * EW:(n + 1) * EW] for n in range(6))
        as_blocks = lambda a: a.rearrange("p (h b j) -> p h b j", h=2, j=J)
        flat = lambda a: a[:, :, :, :].rearrange("p h b j -> p (h b j)")
        keep_w = hot_lo[:, :, :, :].rearrange("p s n c -> p (s n c)")[:, 0:EW]
        blk = lambda i, u: i * U + u

        @block.sync
        def _(sp):
            nload = 0

            def load(o, i):
                nonlocal nload
                sp.dma_start(o, i).then_inc(s_ld, 16)
                nload += 1

            for h, e0 in ((0, 0), (1, BASE1)):
                for to, of in ((dst_i, dst), (src_i, src)):
                    sp.dma_start(as_blocks(to)[:, h, :, :], of[e0:e0 + H].rearrange("(b p j) -> p b j", p=P, j=J))\
                      .then_inc(s_pre, 16)
            half = H // P
            for h, e0 in ((0, 0), (1, BASE1)):
                sp.dma_start(cur_i[:, h * half:(h + 1) * half], dst[e0:e0 + H].rearrange("(p n) -> p n", p=P)).then_inc(s_pre, 16)
            sp.dma_start(prev_i[:, half:2 * half], dst[BASE1 - 1:E - 1].rearrange("(p n) -> p n", p=P)).then_inc(s_pre, 16)
            sp.dma_start(prev_i[1:P, 0:half], dst[half - 1:H - 1].rearrange("(p n) -> p n", n=half)).then_inc(s_pre, 16)
            sp.dma_start(prev_i[0:1, 1:half], dst[0:half - 1].rearrange("(a n) -> a n", a=1)).then_inc(s_pre, 16)
            load(wraw0[:, :], W0)
            load(w1s[:, :], W1)
            load(w2s[:, :], W2)
            load(fcraw[:, :], fcw)
            for l in range(2):
                load(wtop[:, l, :], Wpre[l, 0:F, :])
                load(wbot[:, l, :], Wpre[l, F:2 * F, :])
                load(weS[:, l, :], We[l, :, :])
                load(wlin[:, l, :], Wlin[l, :, :])
                load(wpost[:, l, 0, :], Wpost[l, 0:P, :])
                load(wpost[:, l, 1, :], Wpost[l, P:2 * P, :])
                load(wpost[F:P, l, 2, :], Wpost[l, 2 * P:2 * P + F, :])
                load(wpost[:, l, 3, :], Wpost[l, 2 * P + F:3 * P + F, :])
                load(vecs[:, l, 0:1], be[l, :].rearrange("(c a) -> c a", a=1))
                load(vecs[:, l, 1:2], bpost[l, :].rearrange("(c a) -> c a", a=1))
            for n, v in (("b0", b0), ("b1", b1), ("b2", b2), ("fcb", fcb), ("bn2w", bn2w), ("bn2b", bn2b)):
                load(B[n][:, :], v.rearrange("(a c) -> a c", a=1).broadcast_to([P, v.shape[0]]))
            for n, v in (("bpre", bpre), ("blin", blin), ("gamma", gamma), ("beta", beta)):
                load(B[n][:, :], v.rearrange("(a l) c -> a (l c)", a=1).broadcast_to([P, 2 * F]))
            for part in range(2):
                for h in range(2):
                    at = slice(h * F, h * F + F)
                    load(bnw_c[at, part:part + 1], bn1w[part * F:part * F + F].rearrange("(c a) -> c a", a=1))
                    load(bnb_c[at, part:part + 1], bn1b[part * F:part * F + F].rearrange("(c a) -> c a", a=1))
            sp.wait_ge(s_zero, 1)
            load(xres[:, 0:NT - 1, :], x[0:(NT - 1) * P, :].rearrange("(w p) c -> p w c", p=P))
            load(xres[0:LAST, NT - 1, :], x[(NT - 1) * P:N, :])
            assert nload * 16 == LOADED

            sp.wait_ge(s_wc, 1)
            for l in range(2):
                for j in range(J):
                    for h in range(2):
                        r = h * F + j * 16
                        sp.dma_start(wblk[r:r + 16, l, j, h * F:h * F + F], cS[:, l, :]).then_inc(s_wd, 16)
            sp.dma_start(mid_i[:, :], dst[H:H + 1].rearrange("(a n) -> a n", a=1).broadcast_to([2, 1])).then_inc(s_mi, 16)
            sp.wait_ge(s_kw, 1)
            for h in range(2):
                sp.dma_start(keep_d[h, :].rearrange("(p n) -> p n", p=P), keep_w[:, h * half:(h + 1) * half]).then_inc(s_kd, 16)
            sp.wait_ge(s_kd, 32)

            def attr_load(p, i, u):
                b = blk(i, u)
                if p == MSG and u % 2 == 0:
                    s_abs.done(sp, p, i, u, back=U - 1)
                    for h in range(2):
                        for part in range(2):
                            sp.dma_start(totals[h * F:h * F + F, u:u + 2, part * BLK:(part + 1) * BLK],
                                         total_d[bass.ds(b, 2), part * F:part * F + F, h, :]
                                         .rearrange("a c n -> c a n")).then_inc(s_att.sems[u + part], 16)
                if p not in (SOFT, STAT, *PNA):
                    return
                s_col.done(sp, p, i, u, back=2)
                for h, e0 in ((0, 0), (1, BASE1)):
                    rows = bass.ds(b * BLK + e0, BLK)
                    if p == SOFT:
                        to = attr[:, u % 2, 0:2 * J * F].rearrange("p (j h c) -> p j h c", j=J, h=2)[:, :, h, :]
                        of = ea64[rows, :].rearrange("(p j) c -> p j c", j=J)
                    elif p == STAT:
                        to = attr[:, u % 2, h * J * P:(h + 1) * J * P]
                        of = ea128[rows, :].rearrange("(p j) c -> p (j c)", j=J)
                    elif p in PNA:
                        to = attr[:, u % 2, h * F:h * F + F]
                        of = ea16[rows, :].rearrange("(p j) c -> p (j c)", j=J)
                    sp.dma_start(to, of).then_inc(s_att.sems[u], 16)

            def seed_work(p, i, u):
                b = blk(i, u)
                if p in (GCN1, GCN2):
                    r0 = (0, H)[p == GCN2]
                    sp.dma_start(seed_d[bass.ds(b * BLK + r0, BLK), :].rearrange("(p j) c -> p (j c)", j=J),
                                 attr[:, 0, 0:J * 2 * F]).then_inc(s_zero_out.sems[u], 16)
                elif p == STAT:
                    s_seT.done(sp, p, i, u, back=U)
                    for h in range(2):
                        sp.dma_start(seed[:, u, h, :, :].rearrange("p j c -> p (j c)"),
                                     seed_d[bass.ds(b * BLK + h * H, BLK), :].rearrange("(p j) c -> p (j c)", j=J))\
                          .then_inc(s_sed.sems[u], 16)

            def mask_load(p, i, u):
                if u % 2:
                    return
                s_res.done(sp, p, i, u, back=U - 1)
                if p == STAT:
                    for h, to in enumerate((keep, neg)):
                        sp.dma_start(to[:, u // 2, :],
                                     keep_d[h:h + 1, bass.ds(blk(i, u) * BLK, 2 * BLK)].broadcast_to([P, 2 * BLK]))\
                          .then_inc(s_kee.sems[u], 16)
                    return
                for h in range(2):
                    sp.dma_start(keep[h * F:h * F + F, u // 2, :],
                                 keep_d[h:h + 1, bass.ds(blk(i, u) * BLK, 2 * BLK)].broadcast_to([F, 2 * BLK]))\
                      .then_inc(s_kee.sems[u], 16)

            for p in range(7):
                if p == GCN1:
                    sp.wait_ge(s_at0, 1)
                if p == STAT:
                    s_zero_out.all_done(sp, GCN2)
                    sp.wait_ge(s_td, TABLE[STAT])
                    sp.wait_ge(s_mid, 16)
                    sp.wait_ge(s_sc, 16 * NT)
                    sp.dma_start(seed_d[H + OVER:H + OVER + 1, :], mid_row[0:1, :]).then_inc(s_mi, 16)
                    sp.wait_ge(s_mi, 32)
                if p == MSG:
                    s_out.all_done(sp, STAT)
                    sp.wait_ge(s_wc, 3)
                for u in range(U):
                    mask_load(p, 0, u)
                    seed_work(p, 0, u)
                    attr_load(p, 0, u)
                with sp.Fori(1, IT) as i:
                    for u in range(U):
                        if p == MSG:
                            attr_load(p, i, u)
                            mask_load(p, i, u)
                        else:
                            mask_load(p, i, u)
                            seed_work(p, i, u)
                            attr_load(p, i, u)
                if p == STAT:
                    s_out.all_done(sp, STAT)
                    sp.dma_start(eT[:, 0, 0:BLK - SKIP], total_d[OVER // BLK, :, 1, SKIP:BLK]).then_inc(s_t1, 16)
                    continue
                s_out.all_done(sp, p)
                r, k = (runs3_d, 3) if UNITS[p] == 3 else (runs1_d, 1)
                if p > 0:
                    sp.wait_ge(s_free, ENDS.index(p))
                sp.dma_start(row0[:, 0:k * F], r[H - 1:H, :].broadcast_to([P, k * F])).then_inc(s_r0, 16)
                for q, (a, z) in enumerate(SPAN):
                    rows = slice(a * P, z * P)
                    sp.wait_ge(s_tb, ENDS.index(p) * Q + q + 1)
                    if p == GCN2:
                        tables = ((tsrc_d, feat[:, a:z, 0:2 * F]), (tdst_d, feat[:, a:z, 2 * F:4 * F]))
                    elif p != PNA2:
                        tables = ((table_d[{SOFT: 0, GCN1: 1, MSG: 2, PNA1: 3}[p]], tab[:, a:z, :]),)
                    elif q < Q - 1:
                        tables = ((out, tab[:, a:z, :]),)
                    else:
                        tables = ()
                        sp.dma_start(out[a * P:(z - 1) * P, :].rearrange("(w p) c -> p w c", p=P), tab[:, a:z - 1, :]).then_inc(s_td, 16)
                        sp.dma_start(out[(z - 1) * P:N, :], tab[0:LAST, z - 1, :]).then_inc(s_td, 16)
                    for to, of in tables:
                        sp.dma_start(to[rows, :].rearrange("(w p) c -> p w c", p=P), of).then_inc(s_td, 16)
            sp.wait_ge(s_td, TABLE[PNA2] + 16 * (Q + 1))

        @block.gpsimd
        def _(g):
            g.memset(ident[:, :], 1.0).then_inc(s_c, 1)
            g.memset(tri[:, :], 1.0).then_inc(s_c, 1)
            g.memset(ones[:, :], 1.0).then_inc(s_c, 1)
            g.memset(onesN[:, :], 1.0 / N).then_inc(s_c, 1)
            g.memset(valid[:, :], 1.0).then_inc(s_c, 1)
            g.iota(iota[:, :], pattern=[[1, P]], base=0, channel_multiplier=0,
                   allow_small_or_imprecise_dtypes=True).then_inc(s_c, 1)
            g.wait_ge(s_c, 6)
            g.affine_select(out=ident[:, :], in_=ident[:, :], compare_op=ALU.is_equal, fill=0.0, base=0,
                            pattern=[[-1, P]], channel_multiplier=1).then_inc(s_c, 1)
            g.affine_select(out=tri[:, :], in_=tri[:, :], compare_op=ALU.is_ge, fill=0.0, base=0,
                            pattern=[[1, P]], channel_multiplier=-1).then_inc(s_c, 1)
            g.affine_select(out=valid[:, :], in_=valid[:, :], compare_op=ALU.is_ge, fill=0.0, base=LAST - 1,
                            pattern=[[0, 1]], channel_multiplier=-1).then_inc(s_c, 1)

            FIRST_TILES = [a for a, _ in SPAN]

            def rows(p, i, u):
                s_idx.done(g, p, i, u)
                s_col.done(g, p, i, u, back=U)
                g.sem_inc(s_go, 1)
                table = {SOFT: x, GCN1: table_d[0], GCN2: table_d[1], STAT: tsrc_d,
                         PNA1: table_d[2], PNA2: table_d[3]}[p]
                for h in range(2):
                    for j in range(J):
                        to = gat[:, u, j, h, :] if p == STAT else gat1[:, u, (j * 2 + h) * F:(j * 2 + h + 1) * F]
                        idx = idx_src[:, u, h * J + j:h * J + j + 1]
                        g.indirect_dma_start(out=to, out_offset=None, in_=table,
                                             in_offset=bass.IndirectOffsetOnAxis(ap=idx, axis=0))\
                         .then_inc(s_gat.sems[u], 16)

            for p in range(7):
                if p != MSG:
                    if p == STAT:
                        for q in (GCN1, GCN2):
                            s_zero_out.all_done(g, q)
                        for w in range(NT):
                            if w in FIRST_TILES:
                                g.wait_ge(s_tb, ENDS.index(GCN2) * Q + FIRST_TILES.index(w) + 1)
                            g.indirect_dma_start(out=seed_d, out_offset=bass.IndirectOffsetOnAxis(ap=starti[:, w:w + 1], axis=0),
                                                 in_=feat[:, w, 2 * F:4 * F], in_offset=None,
                                                 bounds_check=2 * H - 1, oob_is_err=False).then_inc(s_sc, 16)
                    if p != SOFT:
                        g.wait_ge(s_td, TABLE[p])
                    if p == STAT:
                        g.wait_ge(s_mi, 16)
                        g.indirect_dma_start(out=mid_row[:, :], out_offset=None, in_=tdst_d,
                                             in_offset=bass.IndirectOffsetOnAxis(ap=mid_i[:, 0:1], axis=0)).then_inc(s_mid, 16)
                    for u in range(U):
                        rows(p, 0, u)
                    with g.Fori(1, IT) as i:
                        for u in range(U):
                            rows(p, i, u)
                if p == STAT:
                    continue
                g.wait_ge(s_end, 1)
                s_out.all_done(g, p)
                if p > 0:
                    g.wait_ge(s_free, ENDS.index(p))
                r, k = (runs3_d, 3) if UNITS[p] == 3 else (runs1_d, 1)
                for w in range(NT):
                    g.indirect_dma_start(out=feat[:, w, F:F + k * F], out_offset=None, in_=r,
                                         in_offset=bass.IndirectOffsetOnAxis(ap=endi[:, w:w + 1], axis=0))\
                     .then_inc(s_endg[sum(w >= z for _, z in SPAN)], 16)

        @block.tensor
        def _(pe):
            mm = nc.tensor.matmul
            pe.wait_ge(s_c, 9)
            pe.wait_ge(s_ld, LOADED)
            def tp(o, i, k):
                return nc.tensor.transpose(o, i, ident[0:k, 0:k])
            pe.wait_ge(s_wp, 1)
            tp(pm[0:F, 0, 0:F], wraw0[:, :], F)
            tp(pm[0:F, 0, F:F + P], fcraw[:, 0:F], P)
            tp(pm[0:F, 0, F + P:F + 2 * P], fcraw[:, F:2 * F], P)
            for l in range(2):
                tp(pm[0:F, 0, 2 * P + F + 16 * l:2 * P + F + 16 * l + 16], weS[:, l, :], 16)
            tp(pm[:, 1, 0:P], fcraw[:, 2 * F:4 * F], P)
            for l in range(2):
                for c in range(4):
                    last = tp(pt[0:F, l, c * P:(c + 1) * P], wpost[:, l, c, :], P)
            last.then_inc(s_w, 1)
            pe.wait_ge(s_wp, 2)
            for l in range(2):
                for c in range(4):
                    mm(pe_[:, l, c * F:(c + 1) * F], wpostT[:, l, c, :], wlin[:, l, :], start=True, stop=True)
                mm(pe_[:, l, 4 * F:5 * F], vecb[:, l, 1, :], wlin[:, l, :], start=True, stop=True)
                mm(pe_[:, l, 5 * F:6 * F], vecb[:, l, 0, :], wbot[:, l, :], start=True, stop=True)
                last = mm(pe_[0:16, l, 6 * F:7 * F], weST[:, l, :], wbot[:, l, :], start=True, stop=True)
            last.then_inc(s_w, 1)
            pe.wait_ge(s_wc, 1)
            pe.wait_ge(s_wd, 16 * 16)

            def turn_features(p, i, u):
                if p not in (STAT, *PNA):
                    return
                s_att.done(pe, p, i, u)
                s_eC.done(pe, p, i, u, back=1)
                if p == STAT:
                    for h in range(2):
                        for j in range(J):
                            last = nc.tensor.transpose(pe_[:, h, j:BLK:J], attr[:, u % 2, (h * J + j) * P:(h * J + j + 1) * P], ident[:, :])
                else:
                    last = nc.tensor.transpose(pe_[:, 0, 0:P], attr[:, u % 2, 0:P], ident[:, :])
                last.then_inc(s_eT.sems[u], 1)

            def columns(p, i, u):
                if p == MSG:
                    return
                s = u % 2
                s_gat.done(pe, p, i, u)
                s_cus.done(pe, p, i, u, back=2)
                if p == SOFT:
                    s_att.done(pe, p, i, u)
                if p in (STAT, *PNA):
                    s_eC.done(pe, p, i, u)
                if p == STAT:
                    for h in range(2):
                        to = (pm[:, h, :], pt[:, 1 + h, :])[s]
                        mm(to, weT[:, :], eT[:, s, h * BLK:(h + 1) * BLK], start=True, stop=False, skip_group_check=True)
                        for j in range(J):
                            last = mm(to[:, j:BLK:J], gat[:, u, j, h, :], ident[:, :],
                                      start=False, stop=True, skip_group_check=True)
                else:
                    for j in range(J):
                        to = pm[:, s, j:BLK:J]
                        if p == SOFT:
                            mm(to, attr[:, u % 2, j * P:(j + 1) * P], ident[:, :], start=True, stop=False, skip_group_check=True)
                        if p in PNA:
                            mm(to, wblk[:, PNA.index(p), j, :], eT[:, s, 0:P], start=True, stop=False, skip_group_check=True)
                        last = mm(to, gat1[:, u, j * P:(j + 1) * P], ident[:, :],
                                  start=(p in (GCN1, GCN2)), stop=True, skip_group_check=True)
                last.then_inc(s_col.sems[u], 1)

            def turn_seeds(p, i, u):
                if p != STAT:
                    return
                s_sed.done(pe, p, i, u)
                s_res.done(pe, p, i, u, back=1)
                for h in range(2):
                    for j in range(J):
                        last = nc.tensor.transpose((pt[:, 0, :], ph[:, :])[h][:, j:BLK:J], seed[:, u, h, j, :], ident[:, :])
                last.then_inc(s_seT.sems[u], 1)

            def turn_back(p, i, u):
                if p == SOFT:
                    s_hot.done(pe, p, i, u)
                    for n in range(2 * J):
                        last = mm(ph[:, 0:NT], hot_lo[:, u % 2, n, :], hot_hi[:, u % 2, n, :],
                                  start=False, stop=False, skip_group_check=True)
                    last.then_inc(s_hus.sems[u], 1)
                if p == STAT:
                    return
                s_res.done(pe, p, i, u)
                s_rev.done(pe, p, i, u, back=1)
                for k in range(UNITS[p]):
                    for j in range(J):
                        last = nc.tensor.transpose(pt[:, k, j * P:(j + 1) * P], res[:, u % 2, k, 1 + j:1 + BLK:J], ident[:, :])
                last.then_inc(s_row.sems[u], 1)

            small = 0

            def small_product(n, o, w, v):
                pe.wait_ge(s_p2s, n)
                mm(o, w, v, start=True, stop=True).then_inc(s_p2d, 1)

            def node_matmuls(*calls):
                steps = [n for n, (job, g, c) in enumerate(STEPS) if JOBS[job][0] in calls]

                def turn(n):
                    job, gr, c = STEPS[n]
                    rows_, width = CALLS[JOBS[job][0]][0:2]
                    if n == 0 or STEPS[n - 1][0] != job:
                        pe.wait_ge(s_in, job + 1)
                    if n >= 2:
                        pe.wait_ge(s_tc, n - 1)
                    a, z = GROUPS[gr]
                    for w in range(a, z):
                        last = nc.tensor.transpose(pe_[0:width, n % 2, (w - a) * P:(w - a + 1) * P], rows_(w, c), ident[:, :])
                    last.then_inc(s_tr, 1)

                def product(n):
                    job, gr, c = STEPS[n]
                    _, width, chunks, weight, cols = CALLS[JOBS[job][0]]
                    G = fill[job, gr]
                    pe.wait_ge(s_tc, n + 1)
                    if c == 0 and G >= 5:
                        pe.wait_ge(s_po, G - 4)
                    a, z = GROUPS[gr]
                    for w in range(a, z):
                        last = mm(pn[:, G % 5, (w - a) * cols:(w - a + 1) * cols], aT[0:width, n % 2, (w - a) * P:(w - a + 1) * P],
                                  weight(c), start=(c == 0 and w == a), stop=(c == chunks - 1), skip_group_check=True)
                    last.then_inc(s_mm, 1)

                for n in steps:
                    if n == steps[0] or STEPS[n - 1][0] != STEPS[n][0]:
                        turn(n)
                    if n < steps[-1] and STEPS[n + 1][0] == STEPS[n][0]:
                        turn(n + 1)
                    product(n)

            for p in range(7):
                if p == SOFT:
                    pe.wait_ge(s_wc, 2)
                    mm(ph[:, 0:NT], hot_lo[:, 1, 0, :], hot_hi[:, 1, 0, :], start=True, stop=False, skip_group_check=True).then_inc(s_h, 1)
                if p != SOFT:
                    pe.wait_ge(s_po, fills_before[p])
                turn_features(p, 0, 0)
                columns(p, 0, 0)
                turn_features(p, 0, 1)
                turn_seeds(p, 0, 0)

                def body(i, end):
                    for u in range(U):
                        nxt, nx2 = (i + (u + 1) // U, (u + 1) % U), (i + (u + 2) // U, (u + 2) % U)
                        if not (end and u + 1 >= U):
                            columns(p, *nxt)
                        if not (end and u + 2 >= U):
                            turn_features(p, *nx2)
                        if not (end and u + 1 >= U):
                            turn_seeds(p, *nxt)
                        turn_back(p, i, u)

                body(0, False)
                with pe.Fori(1, IT - 1) as i:
                    body(i, False)
                body(IT - 1, True)
                if p == SOFT:
                    pe.wait_ge(s_zero, 2)
                    mm(ph[:, 0:NT], hot_lo[:, 0, 0, :], hot_hi[:, 0, 0, :], start=False, stop=True, skip_group_check=True).then_inc(s_h, 1)
                    pe.wait_ge(s_cnt, 1)
                    mm(ph[:, 64:64 + NT], tri[:, :], cnt[:, :], start=True, stop=True)
                    mm(ph[:, 128:128 + NT], ones[:, :], cnt[:, :], start=True, stop=True).then_inc(s_cum, 1)
                    for w in range(NT):
                        pe.wait_ge(s_oh, w + 1)
                        mm(ph[:, 256:256 + NT], hot_lo[:, w % 2, 0, :], hot_hi[:, w % 2, 0, :],
                           start=(w == 0), stop=(w == NT - 1), skip_group_check=True).then_inc(s_ohm, 1)
                    small_product(1, ph[:, 384:385], ones[:, :], col1[:, 0:1])
                    node_matmuls(0, 1)
                elif p == GCN1:
                    node_matmuls(2)
                elif p == GCN2:
                    node_matmuls(3, 4)
                elif p == STAT:
                    pe.wait_ge(s_p2s, 2)
                    for h in range(2):
                        for part in range(2):
                            last = mm(ph[h * F:h * F + F, 2 * part:2 * part + 2], ident[:, part * F:part * F + F], agg2[:, :],
                                      start=True, stop=True)
                    last.then_inc(s_bn, 1)
                elif p == MSG:
                    small_product(3, ph[:, 0:F], onesN[:, :], nrow[:, 0, :])
                    small_product(4, ph[:, F:2 * F], onesN[:, :], nrow[:, 1, :])
                    node_matmuls(5)
                elif p == PNA1:
                    node_matmuls(6)
                    small_product(5, ph[:, 0:F], onesN[:, :], nrow[:, 0, :])
                    small_product(6, ph[:, F:2 * F], onesN[:, :], nrow[:, 1, :])
                    node_matmuls(7)
                elif p == PNA2:
                    node_matmuls(8)
                    small_product(7, ph[:, 0:F], onesN[:, :], nrow[:, 0, :])
                    small_product(8, ph[:, F:2 * F], onesN[:, :], nrow[:, 1, :])

        @block.scalar
        def _(act):
            A = nc.scalar.activation

            def masks(p, i, u):
                if p not in (SOFT, *PNA) or u % 2:
                    return
                v = u // 2
                s_kee.done(act, p, i, u)
                s_res.done(act, p, i, u, back=U - 1)
                if p in PNA:
                    A(pos[:, v, :], keep[:, v, :], ACT.Copy, scale=-BIG, bias=BIG)
                A(neg[:, v, :], keep[:, v, :], ACT.Copy, scale=BIG, bias=-BIG).then_inc(s_neg.sems[u], 1)

            def rows_out(p, i, u):
                s_row.done(act, p, i, u)
                s_out.done(act, p, i, u, back=2)
                K, s = UNITS[p], u % 2
                to = obuf[:, s, 0:2 * J * K * F]
                for k in range(K):
                    last = A(to.rearrange("p (h j k c) -> p k j h c", h=2, j=J, k=K)[:, k, :, :, :],
                             pt[:, k, :].rearrange("p (j h c) -> p j h c", j=J, h=2), ACT.Copy)
                last.then_inc(s_rev.sems[u], 1)
                s_rev.done(act, p, i, u)
                r = runs3_d if K == 3 else runs1_d
                act.dma_start(r.rearrange("(h n) c -> h n c", h=2)[:, bass.ds(blk(i, u) * BLK, BLK), :]
                              .rearrange("h (p j) c -> p h (j c)", j=J),
                              to.rearrange("p (h q) -> p h q", h=2)).then_inc(s_out.sems[u], 16)

            def features(p, i, u):
                s_eT.done(act, p, i, u)
                s_col.done(act, p, i, u, back=2)
                s = u % 2
                if p == STAT:
                    A(eT[:, s, :], pe_[:, :, :].rearrange("p h n -> p (h n)"), ACT.Copy).then_inc(s_eC.sems[u], 1)
                else:
                    A(eT[:, s, 0:P], pe_[:, 0, 0:P], ACT.Copy).then_inc(s_eC.sems[u], 1)

            def logs(i, u):
                s_abs.done(act, MSG, i, u)
                A(ebuf[:, u, :], ebuf[:, u, :], ACT.Exp, scale=-1.0).then_inc(s_e1.sems[u], 1)
                s_e1.done(act, MSG, i, u)
                A(ebuf[:, u, :], ebuf[:, u, :], ACT.Ln, bias=1.0).then_inc(s_ln.sems[u], 1)

            def gate(i, u):
                s_sp.done(act, MSG, i, u)
                A(zbuf[:, u, 0:BLK], zbuf[:, u, 0:BLK], ACT.Exp).then_inc(s_sg.sems[u], 1)

            def body(p, i, end):
                for u in range(U):
                    nxt, nx2 = (i + (u + 1) // U, (u + 1) % U), (i + (u + 2) // U, (u + 2) % U)
                    if p in (STAT, *PNA) and not (end and u + 2 >= U):
                        features(p, *nx2)
                    masks(p, i, u)
                    s = u % 2
                    if p == SOFT:
                        s_dif.done(act, p, i, u)
                        A(expd[:, s, :], dif[:, s, :], ACT.Exp).then_inc(s_exp.sems[u], 1)
                    if p == STAT:
                        s_cus.done(act, p, i, u)
                        act.dma_start(total_d[bass.ds(blk(i, u), 1), :, :, :].rearrange("a p h n -> (a p) (h n)"),
                                      expd[:, s, :]).then_inc(s_out.sems[u], 16)
                        continue
                    if p == MSG:
                        if not (end and u + 2 >= U):
                            logs(*nx2)
                        if not (end and u + 1 >= U):
                            gate(*nxt)
                        if u > 0:
                            rows_out(p, i, u - 1)
                        elif not (isinstance(i, int) and i == 0):
                            rows_out(p, i - 1, U - 1)
                        continue
                    rows_out(p, i, u)

            def node_copies(job):
                for n, (j, gr, c) in enumerate(STEPS):
                    if j != job:
                        continue
                    act.wait_ge(s_tr, n + 1)
                    if n >= 2:
                        act.wait_ge(s_mm, n - 1)
                    width, cols = CALLS[JOBS[j][0]][1], (GROUPS[gr][1] - GROUPS[gr][0]) * P
                    A(aT[0:width, n % 2, 0:cols], pe_[0:width, n % 2, 0:cols], ACT.Copy).then_inc(s_tc, 1)

            asked = 0

            def small(o, i, f, **kw):
                nonlocal asked
                asked += 1
                act.wait_ge(s_a2s, asked)
                A(o, i, f, **kw).then_inc(s_a2d, 1)

            act.wait_ge(s_wc, 1)
            for p in range(7):
                if p in (STAT, *PNA):
                    features(p, 0, 0)
                    features(p, 0, 1)
                if p == MSG:
                    act.preload_act_table_set("natural_log_exp_and_others")
                    logs(0, 0)
                    logs(0, 1)
                    gate(0, 0)
                body(p, 0, False)
                with act.Fori(1, IT - 1) as i:
                    body(p, i, False)
                body(p, IT - 1, True)
                if p == MSG:
                    rows_out(p, IT - 1, U - 1)
                if p == SOFT:
                    small(amp[:, :], mu[:, :], ACT.Ln)
                    small(mu[:, :], var[:, :], ACT.Ln, bias=1.0)
                calls = {SOFT: (0, 1), GCN1: (2,), GCN2: (3, 4), STAT: (), MSG: (5,), PNA1: (6, 7), PNA2: (8,)}[p]
                def exponentials(q):
                    a, z = SPAN[q]
                    both = arena[:, 0:2 * NT * F].rearrange("p (m w c) -> p m w c", m=2, c=F)[:, :, a:z, :]\
                        .rearrange("p m w c -> p m (w c)")
                    small(both, both, ACT.Exp)

                if p == SOFT:
                    exponentials(0)
                for job in of_calls(*calls):
                    k, q = JOBS[job]
                    a, z = SPAN[q]
                    if k == 5:
                        small(tmp2[:, a:z, :], tmp2[:, a:z, :], ACT.Exp)
                        small(tmp2[:, a:z, :], tmp2[:, a:z, :], ACT.Ln, bias=1.0)
                    node_copies(job)
                    if k == 0 and q < Q - 1:
                        exponentials(q + 1)

        @block.vector
        def _(dve):
            V = nc.vector
            TT, TS, STT, SCAN = V.tensor_tensor, V.tensor_scalar, V.scalar_tensor_tensor, V.tensor_tensor_scan
            chain = 0

            def link(ins):
                nonlocal chain
                chain += 1
                ins.then_inc(s_dve, 1)
                dve.wait_ge(s_dve, chain)

            asked = [0, 0]

            def ask_scalar():
                asked[0] += 1
                dve.sem_inc(s_a2s, 1)
                dve.wait_ge(s_a2d, asked[0])

            def ask_tensor():
                asked[1] += 1
                dve.sem_inc(s_p2s, 1)
                dve.wait_ge(s_p2d, asked[1])

            link(V.memset(xres[:, NT - 1, :], 0.0))
            dve.sem_inc(s_zero, 1)
            link(V.memset(wpost[0:F, :, 2, :], 0.0))
            link(V.memset(wblk[:, :, :, :], 0.0))
            dve.wait_ge(s_ld, LOADED)
            link(V.tensor_copy(vecb[:, :, :, :], vecs[:, :, :].unsqueeze(3).broadcast_to([F, 2, 2, P])))
            dve.sem_inc(s_wp, 1)

            dve.wait_ge(s_pre, 9 * 16)
            link(V.memset(prev_i[0:1, 0:1], 0))
            link(TT(keep_w, cur_i, prev_i, ALU.is_equal))
            link(V.memset(keep_w[0:1, 0:1], 0.0))
            link(V.memset(keep_w[0:1, H // P:H // P + 1], 0.0))
            link(V.memset(keep_w[0:1, H // P + OVER:H // P + OVER + 1], 0.0))
            dve.sem_inc(s_kw, 1)

            def copy_indices(p, i, u, new):
                b = new
                last = TS(idx_src[:, u, :].rearrange("p (h j) -> p h j", h=2), src_all[:, :, bass.ds(b, 1), :].rearrange("p h a j -> p h (a j)"), 0.0, None, ALU.add)
                last.then_inc(s_idx.sems[u], 1)

            link(V.tensor_copy(flat(src_all), src_i))
            for u in range(U):
                copy_indices(SOFT, 0, u, u)
            link(TS(lo_i, dst_i, P - 1, None, ALU.bitwise_and))
            link(TS(hi_i, dst_i, 7, None, ALU.logical_shift_right))
            link(V.tensor_copy(flat(dlo), lo_i))
            link(V.tensor_copy(flat(dhi), hi_i))
            link(V.memset(dhi[:, 1, 0:1, :], float(P)))
            link(V.memset(dhi[0:SKIP // J, 1, 1:2, :], float(P)))

            dve.wait_ge(s_w, 1)
            link(V.tensor_copy(w0T[:, :], pm[0:F, 0, 0:F]))
            link(V.tensor_copy(wdT[:, :], pm[0:F, 0, F:F + P]))
            link(V.tensor_copy(wsT[:, :], pm[0:F, 0, F + P:F + 2 * P]))
            link(V.tensor_copy(weST[:, :, :].rearrange("c l k -> c (l k)"), pm[0:F, 0, 2 * P + F:2 * P + F + 32]))
            link(V.tensor_copy(weT[:, :], pm[:, 1, 0:P]))
            for l in range(2):
                link(V.tensor_copy(wpostT[:, l, :, :].rearrange("c n q -> c (n q)"), pt[0:F, l, :]))
            dve.sem_inc(s_wp, 1)
            dve.wait_ge(s_w, 2)
            for l in range(2):
                for c in range(2):
                    for k in range(2):
                        link(V.tensor_copy(wcomb[:, l, c, k * F:(k + 1) * F], pe_[:, l, (2 * k + c) * F:(2 * k + c + 1) * F]))
                v = slice(l * F, l * F + F)
                link(TT(B["blin"][:, v], pe_[:, l, 4 * F:5 * F], B["blin"][:, v], ALU.add))
                link(TT(B["bpre"][:, v], pe_[:, l, 5 * F:6 * F], B["bpre"][:, v], ALU.add))
                link(V.tensor_copy(cS[:, l, :], pe_[0:16, l, 6 * F:7 * F]))
            dve.sem_inc(s_wc, 1)
            dve.wait_ge(s_kd, 32)
            for s in range(2):
                link(V.memset(hot_lo[:, s, 0, :], 0.0))
                link(V.memset(hot_hi[:, s, 0, :], 0.0))
            dve.sem_inc(s_wc, 1)
            dve.wait_ge(s_h, 1)

            def scan(p, u, k, mask, data, mul=False, low=False):
                s = u % 2
                return SCAN(res[:, s, k, 1:BLK + 1], mask, data, res[:, 1 - s, k, BLK:BLK + 1],
                            ALU.mult if mul else ALU.add, ALU.add if mul else ALU.min if low else ALU.max)

            def chained_on(p, i, u, n, ins):
                ins.then_inc(s_lk.sems[u], 1)
                dve.wait_ge(s_lk.sems[u], i * s_lk.adds[p] + (s_lk.base[p] + n))

            def scaled(i, u):
                s_att.done(dve, MSG, i, u - u % 2)
                s_att.done(dve, MSG, i, u - u % 2 + 1)
                TS(zbuf[:, u, 0:BLK], totals[:, u, 0:BLK], bnsc[:, 0:1], bnbi[:, 0:1], ALU.mult, ALU.add)
                chained_on(MSG, i, u, 1, TS(zbuf[:, u, BLK:], totals[:, u, BLK:2 * BLK], bnsc[:, 1:2], bnbi[:, 1:2],
                                            ALU.mult, ALU.add))
                TS(ebuf[:, u, :].bitcast(i32), zbuf[:, u, :].bitcast(i32), 0x7fffffff, None, ALU.bitwise_and).then_inc(s_abs.sems[u], 1)

            def softplus(i, u):
                s_ln.done(dve, MSG, i, u)
                STT(zbuf[:, u, 0:BLK], zbuf[:, u, 0:BLK], 0.0, ebuf[:, u, 0:BLK], ALU.min, ALU.subtract).then_inc(s_sp.sems[u], 1)
                chained_on(MSG, i, u, 2, STT(msg[:, u, :], zbuf[:, u, BLK:], 0.0, ebuf[:, u, BLK:], ALU.max, ALU.add))

            def step(p, i, u, end):
                s, v, half = u % 2, u // 2, slice((u % 2) * BLK, (u % 2) * BLK + BLK)
                nlink = 0 if p != MSG else 2

                def chained(ins):
                    nonlocal nlink
                    nlink += 1
                    chained_on(p, i, u, nlink, ins)

                if p in GATHER:
                    s_col.done(dve, p, i, u)
                    if not end:
                        copy_indices(p, i, u, i * U + (u + U))
                if p == MSG:
                    if not (end and u + 2 >= U):
                        scaled(i + (u + 2) // U, (u + 2) % U)
                    if not (end and u + 1 >= U):
                        softplus(i + (u + 1) // U, (u + 1) % U)
                if p in SCANS:
                    s_row.done(dve, p, i, u, back=2)
                    s_res.done(dve, p, i, u, back=1)
                if p in (SOFT, *PNA):
                    s_neg.done(dve, p, i, u - u % 2)
                else:
                    s_kee.done(dve, p, i, u - u % 2)
                col = pm[:, s, :]
                if p in (GCN1, GCN2):
                    last = scan(p, u, 0, keep[:, v, half], col, mul=True)
                    last.then_inc(s_res.sems[u], 1)
                    s_res.done(dve, p, i, u)
                    dve.sem_inc(s_cus.sems[u], 1)
                elif p in PNA:
                    scan(p, u, 0, keep[:, v, half], col, mul=True)
                    scan(p, u, 1, pos[:, v, half], col, low=True)
                    scan(p, u, 2, neg[:, v, half], col).then_inc(s_res.sems[u], 1)
                    s_res.done(dve, p, i, u)
                    dve.sem_inc(s_cus.sems[u], 1)
                elif p == SOFT:
                    V.tensor_copy(res[:, s, 0, 0:1], res[:, 1 - s, 0, BLK:BLK + 1])
                    chained(scan(p, u, 0, neg[:, v, half], col))
                    R = res[:, s, 0, 1:BLK + 1]
                    chained(TT(dif[:, s, 0:BLK], res[:, s, 0, 0:BLK], neg[:, v, half], ALU.add))
                    TT(dif[:, s, BLK:], col, R, ALU.subtract)
                    TT(dif[:, s, 0:BLK], dif[:, s, 0:BLK], R, ALU.subtract).then_inc(s_dif.sems[u], 1)
                    s_hus.done(dve, p, i, u, back=2)
                    for hot, part, n in ((hot_lo, dlo, P), (hot_hi, dhi, NT)):
                        last = TT(hot[:, s, :, :].rearrange("p (h j) c -> p h j c", h=2),
                                  part[:, :, bass.ds(i * U + u, 1), :].rearrange("p h a j -> p h (a j)").unsqueeze(3).broadcast_to([P, 2, J, n]),
                                  iota[:, 0:n].unsqueeze(1).unsqueeze(1).broadcast_to([P, 2, J, n]), ALU.is_equal)
                    last.then_inc(s_hot.sems[u], 1)
                    s_exp.done(dve, p, i, u)
                    chained(TT(mex[:, :], col, expd[:, s, BLK:], ALU.mult))
                    dve.sem_inc(s_cus.sems[u], 1)
                    scan(p, u, 1, expd[:, s, 0:BLK], expd[:, s, BLK:], mul=True)
                    scan(p, u, 2, expd[:, s, 0:BLK], mex[:, :], mul=True).then_inc(s_res.sems[u], 1)
                    s_res.done(dve, p, i, u)
                elif p == STAT:
                    s_res.done(dve, p, i, u, back=1)
                    s_seT.done(dve, p, i, u)
                    for h in range(2):
                        last = scan(p, u, h, (keep, neg)[h][:, v, half], (pt[:, 0, :], ph[:, :])[h], mul=True)
                    last.then_inc(s_res.sems[u], 1)
                    s_out.done(dve, p, i, u, back=2)
                    s_res.done(dve, p, i, u)
                    for h in range(2):
                        last = TT(expd[:, s, h * BLK:(h + 1) * BLK], (pm[:, h, :], pt[:, 1 + h, :])[s], res[:, s, h, 1:BLK + 1], ALU.add)
                    last.then_inc(s_cus.sems[u], 1)
                    s_cus.done(dve, p, i, u)
                    for h in range(2):
                        V.bn_stats(stats[:, bass.ds(i * U + (u + h * NB), 1), :].rearrange("p a k -> p (a k)"),
                                   expd[:, s, h * BLK:(h + 1) * BLK])
                elif p == MSG:
                    s_sg.done(dve, p, i, u)
                    chained(TT(msg[:, u, :], msg[:, u, :], zbuf[:, u, 0:BLK], ALU.mult))
                    scan(p, u, 0, keep[:, v, half], msg[:, u, :], mul=True).then_inc(s_res.sems[u], 1)

            def edge_pass(p):
                link(V.memset(res[:, 1, :, BLK:BLK + 1], 0.0))
                if p in GATHER and p != SOFT:
                    for u in range(U):
                        copy_indices(p, 0, u, u)
                if p == MSG:
                    scaled(0, 0)
                    scaled(0, 1)
                    softplus(0, 0)
                for u in range(U):
                    step(p, 0, u, False)
                with dve.Fori(1, IT - 1) as i:
                    for u in range(U):
                        step(p, i, u, False)
                for u in range(U):
                    step(p, IT - 1, u, True)

            over_f = lambda a: a.unsqueeze(2).broadcast_to([P, a.shape[1], F])
            over_w = lambda a, n=NT: a.unsqueeze(1).broadcast_to([P, n, F])
            by_f = lambda a: a.rearrange("p w c -> p c w")
            part = lambda k: feat[:, :, k * F:(k + 1) * F]

            def keep_valid(a):
                link(TS(a[:, NT - 1, :], a[:, NT - 1, :], valid[:, 0:1], None, ALU.mult))

            def rsqrt(v, half, t):
                link(TS(half, v, -0.5, None, ALU.mult))
                link(TS(v.bitcast(i32), v.bitcast(i32), -0.5, float(0x5F3759DF), ALU.mult, ALU.add))
                for _ in range(4):
                    link(TT(t, half, v, ALU.mult))
                    link(TT(t, t, v, ALU.mult))
                    link(STT(v, t, 1.5, v, ALU.add, ALU.mult))

            def layer_norm(a, z, x, t, o):
                x, t, o, m, v = x[:, a:z, :], t[:, a:z, :], o[:, a:z, :], mu[:, a:z], var[:, a:z]
                link(V.reduce_sum(m, x, axis=AX.X))
                link(TS(m, m, 1.0 / F, None, ALU.mult))
                link(TT(x, x, over_f(m), ALU.subtract))
                link(TT(t, x, x, ALU.mult))
                link(V.reduce_sum(v, t, axis=AX.X))
                link(TS(v, v, 1.0 / F, 1e-5, ALU.mult, ALU.add))
                rsqrt(v, m, pre[:, a:z])
                link(TT(o, x, over_f(v), ALU.mult))

            def batch_norm(a, t, w, b):
                keep_valid(a)
                link(V.reduce_sum(nrow[:, 0, :], by_f(a), axis=AX.X))
                ask_tensor()
                link(V.tensor_copy(nrow[:, 3, :], ph[:, 0:F]))
                link(TT(t, a, over_w(nrow[:, 3, :]), ALU.subtract))
                keep_valid(t)
                link(TT(a, t, t, ALU.mult))
                link(V.reduce_sum(nrow[:, 1, :], by_f(a), axis=AX.X))
                ask_tensor()
                link(TS(nrow[:, 2, :], ph[:, F:2 * F], 1e-5, None, ALU.add))
                rsqrt(nrow[:, 2, :], nrow[:, 0, :], nrow[:, 1, :])
                link(TT(nrow[:, 3, :], nrow[:, 2, :], w, ALU.mult))
                link(TT(a, t, over_w(nrow[:, 3, :]), ALU.mult))
                link(TT(a, a, over_w(b), ALU.add))

            rows_stand = lambda: dve.sem_inc(s_in, 1)

            def products(k, q, post):
                job = job_of[k, q]
                for g in range(*PARTS[q]):
                    dve.wait_ge(s_mm, step_of[job, g, CALLS[k][2] - 1] + 1)
                    a, z = GROUPS[g]
                    cols = CALLS[k][4]
                    G = fill[job, g]
                    post(a, z, pn[:, G % 5, 0:(z - a) * cols].rearrange("p (n c) -> p n c", c=cols)).then_inc(s_po, 1)
                dve.wait_ge(s_po, G + 1)

            def table_stands():
                dve.sem_inc(s_tb, 1)

            def pipeline(*stages):
                for t in range(Q + len(stages) - 1):
                    for s, stage in enumerate(stages):
                        if 0 <= t - s < Q:
                            stage(t - s, *SPAN[t - s])

            def ends(p, q):
                n = ENDS.index(p) + 1
                dve.wait_ge(s_endg[q], n * (SPAN[q][1] - SPAN[q][0]) * 16)
                if q == 0:
                    dve.wait_ge(s_r0, n * 16)

            def whole_sum(a, z):
                t, o = tmp[:, a:z, :], part(1)[:, a:z, :]
                link(TT(t, over_w(row0[:, 0:F], z - a), over_f(flag[:, a:z]), ALU.mult))
                link(TT(o, o, t, ALU.add))
                link(TT(o, o, over_f(full[:, a:z]), ALU.mult))

            def table_free(p):
                if p in TABLE:
                    dve.wait_ge(s_td, TABLE[p])

            def counts():
                dve.wait_ge(s_hus.sems[U - 1], s_hus.base[SOFT] + IT)
                link(V.memset(hot_lo[:, 0, 0, :], 0.0))
                link(V.memset(hot_hi[:, 0, 0, :], 0.0))
                dve.sem_inc(s_zero, 1)
                dve.wait_ge(s_h, 2)
                link(V.tensor_copy(cnt[:, :], ph[:, 0:NT]))
                dve.sem_inc(s_cnt, 1)
                dve.wait_ge(s_cum, 1)
                link(V.tensor_copy(pre[:, :], ph[:, 128:128 + NT]))
                link(SCAN(var[:, :], ones[:, 0:NT], pre[:, :], 0.0, ALU.mult, ALU.add))
                link(TT(var[:, :], var[:, :], pre[:, :], ALU.subtract))
                link(TT(endf[:, :], ph[:, 64:64 + NT], var[:, :], ALU.add))
                link(TT(pre[:, :], endf[:, :], cnt[:, :], ALU.subtract))
                link(TS(mu[:, :], pre[:, :], float(H), None, ALU.is_ge))
                link(STT(deghi[:, :], mu[:, :], float(OVER), pre[:, :], ALU.mult, ALU.add))
                link(TS(endf[:, :], endf[:, :], 1.0, 0.0, ALU.subtract, ALU.max))
                link(TS(var[:, :], endf[:, :], float(H), None, ALU.is_ge))
                link(TS(pre[:, :], pre[:, :], float(H), None, ALU.is_lt))
                link(TS(full[:, :], cnt[:, :], 0.0, None, ALU.is_gt))
                link(TT(flag[:, :], pre[:, :], var[:, :], ALU.mult))
                link(TT(flag[:, :], flag[:, :], full[:, :], ALU.mult))
                link(STT(endf[:, :], var[:, :], float(OVER), endf[:, :], ALU.mult, ALU.add))
                link(V.tensor_copy(endi[:, :], endf[:, :]))
                link(TS(mu[:, :], full[:, :], -2.0 ** 20, 2.0 ** 20, ALU.mult, ALU.add))
                link(TT(mu[:, :], mu[:, :], deghi[:, :], ALU.add))
                link(V.tensor_copy(starti[:, :], mu[:, :]))
                dve.sem_inc(s_end, 1)
                link(TS(dinv[:, :], cnt[:, :], 1.0, None, ALU.add))
                rsqrt(dinv[:, :], mu[:, :], var[:, :])
                link(TS(mu[:, :], cnt[:, :], 1.0, 1.0, ALU.max, ALU.add))
                ask_scalar()
                i0, i1 = mu[:, :].bitcast(i32), var[:, :].bitcast(i32)
                link(V.tensor_copy(i0, cnt[:, :]))
                link(TS(i1, i0, P - 1, None, ALU.bitwise_and))
                link(V.tensor_copy(deglo[:, :], i1))
                link(TS(i1, i0, 7, None, ALU.logical_shift_right))
                link(V.tensor_copy(deghi[:, :], i1))
                link(TS(col1[:, 0:1], valid[:, 0:1], -1000.0, 1000.0, ALU.mult, ALU.add))
                link(TT(deghi[:, NT - 1:NT], deghi[:, NT - 1:NT], col1[:, 0:1], ALU.add))
                for w in range(NT):
                    if w >= 2:
                        dve.wait_ge(s_ohm, w - 1)
                    link(TS(hot_lo[:, w % 2, 0, :], iota[:, :], deglo[:, w:w + 1], None, ALU.is_equal))
                    TS(hot_hi[:, w % 2, 0, :], iota[:, 0:NT], deghi[:, w:w + 1], None, ALU.is_equal).then_inc(s_oh, 1)
                dve.wait_ge(s_ohm, NT)
                link(V.tensor_copy(var[:, :], ph[:, 256:256 + NT]))
                ask_scalar()
                link(TT(mu[:, NT - 1:NT], mu[:, NT - 1:NT], valid[:, 0:1], ALU.mult))
                link(V.reduce_sum(col1[:, 0:1], mu[:, :], axis=AX.X))
                ask_tensor()
                link(TS(col1[:, 1:2], ph[:, 384:385], 1.0 / N, None, ALU.mult))
                link(V.reciprocal(col1[:, 1:2], col1[:, 1:2]))
                link(TS(amp[:, :], amp[:, :], col1[:, 1:2], None, ALU.mult))

            def extreme(k, a, z, sign):
                t, m = tmp[:, a:z, :], mu[:, a:z]
                link(TS(m, flag[:, a:z], 1.0, sign * BIG, ALU.subtract, ALU.mult))
                link(TT(t, over_w(row0[:, (k - 1) * F:k * F], z - a), over_f(flag[:, a:z]), ALU.mult))
                link(TT(t, t, over_f(m), ALU.add))

            def scaled_table(k):
                def stage(q, a, z):
                    products(k, q, lambda a, z, o: TT(tab[:, a:z, :], o, over_f(dinv[:, a:z]), ALU.mult))
                    table_stands()
                return stage

            def shifted_table(k, v):
                def stage(q, a, z):
                    products(k, q, lambda a, z, o: TT(tab[:, a:z, :], o, over_w(B["bpre"][:, v], z - a), ALU.add))
                    table_stands()
                return stage

            def node_phase_done():
                dve.sem_inc(s_free, 1)

            def soft_merge(q, a, z):
                ends(SOFT, q)
                t, t2, m = tmp[:, a:z, :], tmp2[:, a:z, :], tab[:, a:z, :]
                R_, D_, A_ = (part(k)[:, a:z, :] for k in (1, 2, 3))
                extreme(1, a, z, 1.0)
                link(TT(m, R_, t, ALU.max))
                link(TT(t2, R_, m, ALU.subtract))
                link(TT(t, t, m, ALU.subtract))
                ask_scalar()
                for k, o in ((2, D_), (3, A_)):
                    link(TT(o, o, t2, ALU.mult))
                    link(TT(m, over_w(row0[:, (k - 1) * F:k * F], z - a), t, ALU.mult))
                    link(TT(o, o, m, ALU.add))
                link(TS(D_, D_, 1e-38, None, ALU.max))
                link(V.reciprocal(t2, D_))
                link(TT(t, A_, t2, ALU.mult))
                link(TT(t, t, over_f(full[:, a:z]), ALU.mult))
                rows_stand()

            def soft_out(q, a, z):
                products(0, q, lambda a, z, o: TT(tmp2[:, a:z, :], o, over_w(B["b0"][:, :], z - a), ALU.add))
                t2, x_ = tmp2[:, a:z, :], xres[:, a:z, :]
                link(STT(t2, t2, 0.0, x_, ALU.max, ALU.add))
                link(TT(t2, t2, x_, ALU.add))
                layer_norm(a, z, tmp2, tmp, xres)
                rows_stand()

            edge_pass(SOFT)
            link(V.memset(attr[:, :, :], 0.0))
            dve.sem_inc(s_at0, 1)
            counts()
            pipeline(soft_merge, soft_out, scaled_table(1))
            node_phase_done()

            def gcn_out(p):
                def stage(q, a, z):
                    ends(p, q)
                    if q == 0:
                        table_free(p)
                    whole_sum(a, z)
                    t = tmp[:, a:z, :]
                    link(TT(t, part(1)[:, a:z, :], tab[:, a:z, :], ALU.add))
                    link(TT(t, t, over_f(dinv[:, a:z]), ALU.mult))
                    link(TT(t, t, over_w(B["b1" if p == GCN1 else "b2"][:, :], z - a), ALU.add))
                    if p == GCN1:
                        link(TS(t, t, 0.0, None, ALU.max))
                        rows_stand()
                    else:
                        link(TT(t, t, xres[:, a:z, :], ALU.add))
                        layer_norm(a, z, tmp, tmp2, xres)
                        rows_stand()
                        rows_stand()
                return stage

            def wide_tables(q, a, z):
                products(3, q, lambda a, z, o: V.tensor_copy(feat[:, a:z, 0:2 * F], o))
                products(4, q, lambda a, z, o: TT(feat[:, a:z, 2 * F:4 * F], o,
                                                  B["fcb"][:, :].unsqueeze(1).broadcast_to([P, z - a, 2 * F]), ALU.add))
                table_stands()

            edge_pass(GCN1)
            pipeline(gcn_out(GCN1), scaled_table(2))
            node_phase_done()
            edge_pass(GCN2)
            pipeline(gcn_out(GCN2), wide_tables)
            node_phase_done()

            edge_pass(STAT)
            dve.wait_ge(s_t1, 16)
            link(V.bn_stats(stats[:, NB + 1, :], eT[:, 0, 0:BLK - SKIP]))
            link(V.tensor_copy(stats[:, NB, :], stats[:, 2 * NB - 1, :]))
            link(V.bn_aggr(agg2[:, :], stats[:, 0:2 * NB - 1, :].rearrange("p n k -> p (n k)")))
            dve.sem_inc(s_p2s, 1)
            dve.wait_ge(s_bn, 1)
            link(V.tensor_copy(nrow[:, 0, 0:4], ph[:, 0:4]))
            link(TS(col1[:, 0:2], nrow[:, 0, 1:4:2], 1e-5, None, ALU.add))
            rsqrt(col1[:, 0:2], col1[:, 2:4], nrow[:, 1, 0:2])
            link(TT(bnsc[:, :], bnw_c[:, :], col1[:, 0:2], ALU.mult))
            link(TT(bnbi[:, :], bnsc[:, :], nrow[:, 0, 0:4:2], ALU.mult))
            link(TT(bnbi[:, :], bnb_c[:, :], bnbi[:, :], ALU.subtract))
            dve.sem_inc(s_wc, 1)

            def msg_sum(q, a, z):
                ends(MSG, q)
                whole_sum(a, z)
                link(V.tensor_copy(tmp[:, a:z, :], part(1)[:, a:z, :]))

            def msg_out(q, a, z):
                t, t2, x_ = tmp[:, a:z, :], tmp2[:, a:z, :], xres[:, a:z, :]
                link(TT(t, t, x_, ALU.add))
                link(STT(t2, t, -1.0, t, ALU.mult, ALU.min))
                ask_scalar()
                ask_scalar()
                link(STT(t, t, 0.0, t2, ALU.max, ALU.add))
                link(TT(t, t, x_, ALU.add))
                layer_norm(a, z, tmp, tmp2, xres)
                link(V.tensor_copy(part(0)[:, a:z, :], x_))
                rows_stand()

            edge_pass(MSG)
            pipeline(msg_sum)
            table_free(MSG)
            batch_norm(tmp[:, :, :], tmp2[:, :, :], B["bn2w"][:, :], B["bn2b"][:, :])
            pipeline(msg_out, shifted_table(5, slice(0, F)))
            node_phase_done()

            def pna_aggregates(p):
                def stage(q, a, z):
                    ends(p, q)
                    whole_sum(a, z)
                    m, one_ = mu[:, a:z], part(1)[:, a:z, :]
                    link(TS(m, cnt[:, a:z], 1.0, None, ALU.max))
                    link(V.reciprocal(m, m))
                    link(TT(one_, one_, over_f(m), ALU.mult))
                    for k, op, sign in ((2, ALU.min, -1.0), (3, ALU.max, 1.0)):
                        o = part(k)[:, a:z, :]
                        extreme(k, a, z, sign)
                        link(TT(o, o, tmp[:, a:z, :], op))
                        link(TT(o, o, over_f(full[:, a:z]), ALU.mult))
                    rows_stand()
                return stage

            def pna_post(k, v):
                def post(a, z, o):
                    link(TT(tmp2[:, a:z, :], o[:, :, F:2 * F], over_f(amp[:, a:z]), ALU.mult))
                    return TT(tmp2[:, a:z, :], tmp2[:, a:z, :], o[:, :, 0:F], ALU.add)

                def stage(q, a, z):
                    products(k, q, post)
                    link(TT(tmp2[:, a:z, :], tmp2[:, a:z, :], over_w(B["blin"][:, v], z - a), ALU.add))
                return stage

            def pna_next(q, a, z):
                link(TS(part(0)[:, a:z, :], tmp2[:, a:z, :], 0.0, None, ALU.max))
                rows_stand()

            def pna_end(q, a, z):
                link(STT(tmp2[:, a:z, :], tmp2[:, a:z, :], 0.0, xres[:, a:z, :], ALU.max, ALU.add))
                layer_norm(a, z, tmp2, tmp, tab)
                table_stands()

            for l, p in enumerate(PNA):
                v = slice(l * F, l * F + F)
                edge_pass(p)
                pipeline(pna_aggregates(p), pna_post(6 if l == 0 else 8, v))
                table_free(p)
                batch_norm(tmp2[:, :, :], tmp[:, :, :], B["gamma"][:, v], B["beta"][:, v])
                if l == 0:
                    pipeline(pna_next, shifted_table(7, slice(F, 2 * F)))
                    node_phase_done()
                else:
                    pipeline(pna_end)


_INS = ["x", "src", "dst", "edge_attr_128", "edge_attr_16", "edge_attr_64", "L0_gnn_W", "L0_gnn_b",
        "L1_gnn_W1", "L1_gnn_b1", "L1_gnn_W2", "L1_gnn_b2", "L2_gnn_fc_w", "L2_gnn_fc_b",
        "L2_gnn_bn1_w", "L2_gnn_bn1_b", "L2_gnn_bn2_w", "L2_gnn_bn2_b", "L3_gnn_We", "L3_gnn_be",
        "L3_gnn_Wpre", "L3_gnn_bpre", "L3_gnn_Wpost", "L3_gnn_bpost", "L3_gnn_Wlin", "L3_gnn_blin",
        "L3_gnn_gamma", "L3_gnn_beta"]


def kernel(**inputs):
    import numpy as _np
    import concourse.bacc as _bacc
    from concourse import mybir as _mybir
    from concourse.bass_utils import run_bass_kernel_spmd as _run

    nc = _bacc.Bacc("TRN2", target_bir_lowering=False, num_devices=1)
    arrays, args = {}, []
    for name in _INS:
        a = _np.ascontiguousarray(inputs[name])
        arrays[f"in_{name}_dram"] = a
        args.append(nc.dram_tensor(f"in_{name}_dram", a.shape, _mybir.dt.from_np(a.dtype), kind="ExternalInput").ap())
    args.append(nc.dram_tensor("out_0_dram", (6250, 64), _mybir.dt.float32, kind="ExternalOutput").ap())
    gnn_kernel(nc, *args)
    r = _run(nc, [arrays], core_ids=[0])
    return r.results[0]["out_0_dram"]
```
